# Optimizing a Trainium2 kernel written in Bass

```python
import numpy as np
import jax
import jax.numpy as jnp

def _softmax(x, axis=-1):
    return jax.nn.softmax(x, axis=axis)

def _gelu(x):
    return jax.nn.gelu(x, approximate=True)

def _silu(x):
    return jax.nn.silu(x)

def _sigmoid(x):
    return jax.nn.sigmoid(x)

def _layernorm(x, axis=-1, eps=1e-05):
    m = jnp.mean(x, axis=axis, keepdims=True)
    v = jnp.var(x, axis=axis, keepdims=True)
    return (x - m) / jnp.sqrt(v + eps)

def _scatter_add(tgt, idx, src, axis=0):
    return tgt.at[idx].add(src)

def _segment_sum(src, seg, n):
    return jax.ops.segment_sum(src, seg, n)
kernel_name = 'mk_sandwich_d1_jaxref_r8_681cf9'

def setup_inputs(seed: int=0):
    np.random.seed(seed)
    _w = jnp.asarray

    def _L0_attn_setup():
        import jax, jax.numpy as jnp
        import numpy as np
        H = 16
        NB = 64
        NH = 6
        key = jax.random.key(seed)
        k = jax.random.split(key, 6)
        E = 128
        B, S = (2, 256)
        return {'x': jax.random.normal(k[0], (B, S, E), jnp.float32), 'Wq': jax.random.normal(k[1], (E, E), jnp.float32) * E ** (-0.5), 'bq': jax.random.normal(k[2], (E,), jnp.float32) * 0.02, 'Wv': jax.random.normal(k[3], (E, E), jnp.float32) * E ** (-0.5), 'bv': jax.random.normal(k[4], (E,), jnp.float32) * 0.02, 'hyperplanes': jax.random.normal(k[5], (E // H + 1, NH), jnp.float32)}
    _L0_attn_in = _L0_attn_setup()

    def _L0_ffn_setup():
        import jax, jax.numpy as jnp
        import numpy as np
        D_IN, D_HID = (128, 512)

        def _ternary(key, shape):
            return jax.random.randint(key, shape, -1, 2).astype(jnp.float32)

        def _tlin(x, w, s):
            return jnp.einsum('bsi,oi->bso', x, w) * s
        key = jax.random.key(seed)
        ks = jax.random.split(key, 12)
        inv = lambda fan: 1.0 / np.sqrt(fan).astype(np.float32)
        return {'x': jax.random.normal(ks[0], (4, 256, D_IN), dtype=jnp.float32), 'w1_w': _ternary(ks[1], (D_HID, D_IN)), 'w1_s': jax.random.uniform(ks[2], (D_HID,), dtype=jnp.float32) * inv(D_IN), 'w2_w': _ternary(ks[3], (D_HID, D_IN)), 'w2_s': jax.random.uniform(ks[4], (D_HID,), dtype=jnp.float32) * inv(D_IN), 'h1_w': _ternary(ks[5], (D_HID, D_HID)), 'h1_s': jax.random.uniform(ks[6], (D_HID,), dtype=jnp.float32) * inv(D_HID), 'h2_w': _ternary(ks[7], (D_HID, D_HID)), 'h2_s': jax.random.uniform(ks[8], (D_HID,), dtype=jnp.float32) * inv(D_HID), 'w3_w': _ternary(ks[9], (D_IN, D_HID)), 'w3_s': jax.random.uniform(ks[10], (D_IN,), dtype=jnp.float32) * inv(D_HID)}
    _L0_ffn_in = _L0_ffn_setup()
    _d = {'L0_attn_x': _L0_attn_in['x'], 'L0_attn_Wq': _L0_attn_in['Wq'], 'L0_attn_bq': _L0_attn_in['bq'], 'L0_attn_Wv': _L0_attn_in['Wv'], 'L0_attn_bv': _L0_attn_in['bv'], 'L0_attn_hyperplanes': _L0_attn_in['hyperplanes'], 'L0_ffn_w1_w': _L0_ffn_in['w1_w'], 'L0_ffn_w1_s': _L0_ffn_in['w1_s'], 'L0_ffn_w2_w': _L0_ffn_in['w2_w'], 'L0_ffn_w2_s': _L0_ffn_in['w2_s'], 'L0_ffn_h1_w': _L0_ffn_in['h1_w'], 'L0_ffn_h1_s': _L0_ffn_in['h1_s'], 'L0_ffn_h2_w': _L0_ffn_in['h2_w'], 'L0_ffn_h2_s': _L0_ffn_in['h2_s'], 'L0_ffn_w3_w': _L0_ffn_in['w3_w'], 'L0_ffn_w3_s': _L0_ffn_in['w3_s']}
    _x0 = _d['L0_attn_x']
    _d['L0_attn_x'] = jax.random.normal(jax.random.fold_in(jax.random.key(seed), 1), (16, 512, 128), dtype=_x0.dtype)
    del _x0
    return _d

def reference(L0_attn_x, L0_attn_Wq, L0_attn_bq, L0_attn_Wv, L0_attn_bv, L0_attn_hyperplanes, L0_ffn_w1_w, L0_ffn_w1_s, L0_ffn_w2_w, L0_ffn_w2_s, L0_ffn_h1_w, L0_ffn_h1_s, L0_ffn_h2_w, L0_ffn_h2_s, L0_ffn_w3_w, L0_ffn_w3_s):

    def _L0_attn_ref(x, Wq, bq, Wv, bv, hyperplanes):
        import jax, jax.numpy as jnp
        import numpy as np
        H = 16
        NB = 64
        NH = 6
        B, S, E = x.shape
        Dh = E // H
        q = (x @ Wq.T + bq).reshape(B, S, H, Dh)
        v = (x @ Wv.T + bv).reshape(B, S, H, Dh)
        qa = jnp.concatenate([q, jnp.ones((B, S, H, 1), q.dtype)], axis=-1)
        proj = jnp.einsum('bshe,en->bshn', qa, hyperplanes)
        bits = (proj >= 0).astype(jnp.int32)
        buckets = jnp.einsum('bshn,n->bsh', bits, 2 ** jnp.arange(NH, dtype=jnp.int32))
        b_hs = buckets.transpose(0, 2, 1)
        q = q.transpose(0, 2, 1, 3)
        v = v.transpose(0, 2, 1, 3)
        scores = jnp.einsum('bhsd,bhtd->bhst', q, q) / jnp.sqrt(jnp.float32(E))
        same = (b_hs[:, :, :, None] == b_hs[:, :, None, :]).astype(scores.dtype)
        coeff = NB - 2 + same
        attn = jax.nn.softmax(scores * coeff, axis=-1)
        out = jnp.einsum('bhst,bhtd->bhsd', attn, v)
        return out.transpose(0, 2, 1, 3).reshape(B, S, E)

    def _L0_ffn_ref(x, w1_w, w1_s, w2_w, w2_s, h1_w, h1_s, h2_w, h2_s, w3_w, w3_s):
        import jax, jax.numpy as jnp
        import numpy as np
        D_IN, D_HID = (128, 512)

        def _ternary(key, shape):
            return jax.random.randint(key, shape, -1, 2).astype(jnp.float32)

        def _tlin(x, w, s):
            return jnp.einsum('bsi,oi->bso', x, w) * s
        h = jax.nn.silu(_tlin(x, w1_w, w1_s)) * _tlin(x, w2_w, w2_s)
        h = jax.nn.gelu(_tlin(h, h1_w, h1_s), approximate=False)
        h = jax.nn.gelu(_tlin(h, h2_w, h2_s), approximate=False)
        return _tlin(h, w3_w, w3_s)
    x = L0_attn_x
    x = x + _layernorm(_L0_attn_ref(_layernorm(x, axis=-1), L0_attn_Wq, L0_attn_bq, L0_attn_Wv, L0_attn_bv, L0_attn_hyperplanes), axis=-1)
    x = x + _layernorm(_L0_ffn_ref(_layernorm(x, axis=-1), L0_ffn_w1_w, L0_ffn_w1_s, L0_ffn_w2_w, L0_ffn_w2_s, L0_ffn_h1_w, L0_ffn_h1_s, L0_ffn_h2_w, L0_ffn_h2_s, L0_ffn_w3_w, L0_ffn_w3_s), axis=-1)
    return x

_drawn_inputs = setup_inputs


def setup_inputs(seed=0):
    import zlib

    import numpy as np

    out = dict(_drawn_inputs(seed))
    spreads = {}
    factors = {'L0_attn_bv': 3.199}
    for name, (base, spread) in spreads.items():
        noise = np.random.default_rng([zlib.crc32(name.encode()), seed]).standard_normal(out[name].shape)
        drawn = base * np.exp(spread * noise) if base else spread * noise
        out[name] = jnp.asarray(drawn.astype(out[name].dtype))
    for name, factor in factors.items():
        out[name] = (out[name] * factor).astype(out[name].dtype)
    return out
```

```python
from contextlib import ExitStack

import concourse.bass as bass
from concourse import mybir

FP32 = mybir.dt.float32
BF16 = mybir.dt.bfloat16
ALU = mybir.AluOpType
ACT = mybir.ActivationFunctionType
AXIS_X = mybir.AxisListType.X

P = 128
E = 128
H = 16
DH = E // H
NH = 6
BUCKETS = 2 ** NH
SEQ = 512
BATCH = 16
HID = 512
ST = SEQ // P
HT = HID // P
QUADS = H // 4
TILES = H * ST
QT = 4 * ST
PARTS = 3
KROWS = PARTS * PARTS * DH
VW = 32
EPS = 1e-5
T_LAG = 3
X_LAG = 4


def sandwich_kernel(nc, x, wqT, bq, wvT, bv, hyper_blocks, hyper_bias, w1T, w2T, h1T, h2T, scales, w3T, w3_s, out):
    ctx = ExitStack()
    with ctx:
        def sb(name, shape, dt=FP32):
            return ctx.enter_context(nc.sbuf_tensor(name, shape, dt))

        def bank(name):
            return ctx.enter_context(nc.psum_tensor(name, [P, SEQ], FP32))

        def sem(name):
            return ctx.enter_context(nc.semaphore(name))

        q_scratch = nc.dram_tensor("q_scratch", [BATCH, PARTS * DH, H * SEQ], BF16, kind="Internal").ap()
        bucket_scratch = nc.dram_tensor("bucket_scratch", [BATCH, H * SEQ], BF16, kind="Internal").ap()

        wq_sb = sb("wq_sb", [P, E])
        wv_sb = sb("wv_sb", [P, E])
        bq_sb = sb("bq_sb", [P, 1])
        bv_sb = sb("bv_sb", [P, E])
        hyper_sb = sb("hyper_sb", [P, NH * H])
        hbias_sb = sb("hbias_sb", [P, NH, H])
        pow2_sb = sb("pow2_sb", [P, NH, H])
        w1_sb = sb("w1_sb", [P, HID])
        w2_sb = sb("w2_sb", [P, HID])
        h1_sb = sb("h1_sb", [P, HT, HID])
        h2_sb = sb("h2_sb", [P, HT, HID])
        w3_sb = sb("w3_sb", [P, HT, E])
        scales_sb = sb("scales_sb", [P, 4, HT])
        w3s_sb = sb("w3s_sb", [P, E])
        ident = sb("ident", [P, P])
        minus_half = sb("minus_half", [P, ST])

        x_in = sb("x_in", [P, ST, E])
        x_stats = sb("x_stats", [P, ST, 6])
        x_mv = sb("x_mv", [P, ST, 2])
        x_var = sb("x_var", [P, ST])
        x_rstd = sb("x_rstd", [P, ST])
        xn = sb("xn", [P, ST, E])
        xnT = sb("xnT", [P, SEQ])
        qT = sb("qT", [P, SEQ])
        q_rest = sb("q_rest", [P, 2, SEQ])
        q_parts = sb("q_parts", [P, PARTS, SEQ], BF16)
        v_next = sb("v_next", [P, ST, H, DH])
        proj = sb("proj", [P, ST, NH, H])
        bits = sb("bits", [P, ST, NH, H])
        bcol_next = sb("bcol_next", [P, ST, H])
        brow16 = sb("brow16", [H, SEQ], BF16)

        stat_stack = sb("stat_stack", [P, 2, 4, SEQ], BF16)
        mov_stack = sb("mov_stack", [P, 2, 4, SEQ], BF16)
        brow = sb("brow", [P, 2, 4, SEQ], BF16)
        bcol = sb("bcol", [P, ST, H])
        coeff = sb("coeff", [P, 3, SEQ], BF16)
        logits = sb("logits", [P, 4, SEQ])
        rowmax = sb("rowmax", [P, TILES])
        below_max = sb("below_max", [P, 4, SEQ])
        probs = sb("probs", [P, 2, 4, ST, SEQ])
        v_pad = sb("v_pad", [P, ST, H, VW])
        oT = sb("oT", [P, SEQ])
        rden = sb("rden", [P, ST, 4])
        att = sb("att", [P, ST, E])

        x_res = sb("x_res", [P, ST, E])
        att_stats = sb("att_stats", [P, ST, 6])
        att_mv = sb("att_mv", [P, ST, 2])
        att_var = sb("att_var", [P, ST])
        att_rstd = sb("att_rstd", [P, ST])
        normed = sb("normed", [P, ST, E])
        y1 = sb("y1", [P, ST, E])
        yn = sb("yn", [P, ST, E])
        ynT = sb("ynT", [P, SEQ])
        gate = sb("gate", [P, 2, SEQ])
        hid_a = sb("hid_a", [P, HT, SEQ])
        hid_b = sb("hid_b", [P, HT, SEQ])
        ffn = sb("ffn", [P, ST, E])
        y2 = sb("y2", [P, ST, E])

        s_bank = [bank(f"s_bank{n}") for n in range(2)]
        t_bank = [bank(f"t_bank{n}") for n in range(2)]
        f_bank = [bank(f"f_bank{n}") for n in range(2)]
        pv_bank = bank("pv_bank")
        aux_bank = bank("aux_bank")

        weights_in = sem("weights_in")
        stacks_clear = sem("stacks_clear")
        consts_made = sem("consts_made")
        x_loaded = sem("x_loaded")
        x_stats_done = sem("x_stats_done")
        x_mv_done = sem("x_mv_done")
        x_var_done = sem("x_var_done")
        x_rstd_done = sem("x_rstd_done")
        xn_done = sem("xn_done")
        xnT_psum = sem("xnT_psum")
        xnT_done = sem("xnT_done")
        q_psum = sem("q_psum")
        q_done = sem("q_done")
        v_psum = sem("v_psum")
        v_next_done = sem("v_next_done")
        proj_psum = sem("proj_psum")
        proj_done = sem("proj_done")
        bits_done = sem("bits_done")
        bcol_next_done = sem("bcol_next_done")
        brow_psum = sem("brow_psum")
        brow_done = sem("brow_done")
        q_part_steps = sem("q_part_steps")
        scratch_written = sem("scratch_written")
        stack_loaded = [sem(f"stack_loaded{n}") for n in range(2)]
        bcol_done = sem("bcol_done")
        v_pad_done = sem("v_pad_done")
        scores_psum = sem("scores_psum")
        coeff_done = sem("coeff_done")
        logits_done = sem("logits_done")
        below_max_done = sem("below_max_done")
        transposed_psum = sem("transposed_psum")
        probs_done = sem("probs_done")
        pv_psum = sem("pv_psum")
        oT_done = sem("oT_done")
        o_psum = sem("o_psum")
        rden_done = sem("rden_done")
        att_done = sem("att_done")
        x_res_loaded = sem("x_res_loaded")
        att_stats_done = sem("att_stats_done")
        att_mv_done = sem("att_mv_done")
        att_var_done = sem("att_var_done")
        att_rstd_done = sem("att_rstd_done")
        normed_done = sem("normed_done")
        y1_done = sem("y1_done")
        yn_done = sem("yn_done")
        ynT_psum = sem("ynT_psum")
        ynT_done = sem("ynT_done")
        w1_psum = sem("w1_psum")
        gate_done = sem("gate_done")
        w2_psum = sem("w2_psum")
        h0_done = sem("h0_done")
        h1_psum = sem("h1_psum")
        h1_done = sem("h1_done")
        h2_psum = sem("h2_psum")
        h2_done = sem("h2_done")
        w3_psum = sem("w3_psum")
        ffn_done = sem("ffn_done")
        y2_done = sem("y2_done")
        out_stored = sem("out_stored")
        waited = sem("waited")

        WEIGHT_DMAS = 13
        x_view = x.rearrange("b (s p) e -> b p s e", p=P)
        out_view = out.rearrange("b (s p) e -> b p s e", p=P)

        def apart(eng):
            eng.sem_inc(waited, 1)

        def begun(b):
            return not isinstance(b, int) or b > 0

        def stages(eng, iteration):
            iteration(-1, project=True, attend=False, feed=False)
            iteration(0, project=True, attend=True, feed=False)
            with eng.Fori(1, BATCH - 1) as i:
                iteration(i, project=True, attend=True, feed=True)
            iteration(BATCH - 1, project=False, attend=True, feed=True)
            iteration(BATCH, project=False, attend=False, feed=True)

        block = ctx.enter_context(nc.Block())

        @block.sync
        def _(sp):
            sp.dma_start(x_in[:], x_view[0]).then_inc(x_loaded, 16)
            for dst, src in (
                (wq_sb[:], wqT), (bq_sb[:], bq.rearrange("(p a) -> p a", a=1)),
                (wv_sb[:], wvT), (bv_sb[:], bv.rearrange("(a e) -> a e", a=1).broadcast_to([P, E])),
                (hyper_sb[:], hyper_blocks),
                (hbias_sb[:].rearrange("p n h -> p (n h)"),
                 hyper_bias.rearrange("(a e) -> a e", a=1).broadcast_to([P, NH * H])),
                (w1_sb[:], w1T), (w2_sb[:], w2T),
                (h1_sb[:], h1T.rearrange("(k p) n -> p k n", p=P)),
                (h2_sb[:], h2T.rearrange("(k p) n -> p k n", p=P)),
                (scales_sb[:], scales),
                (w3_sb[:], w3T.rearrange("(k p) n -> p k n", p=P)),
                (w3s_sb[:], w3_s.rearrange("(a e) -> a e", a=1).broadcast_to([P, E])),
            ):
                sp.dma_start(dst, src).then_inc(weights_in, 16)

            def load_stacks(b, quad):
                slot = quad % 2
                cols = slice(quad * 4 * SEQ, (quad + 1) * 4 * SEQ)
                for i in range(PARTS):
                    sp.dma_start(mov_stack[i * PARTS * DH:(i + 1) * PARTS * DH, slot].rearrange("p h n -> p (h n)"),
                                 q_scratch[b][:, cols]).then_inc(stack_loaded[slot], 16)
                    for j in range(PARTS):
                        row = (i * PARTS + j) * DH
                        sp.dma_start(stat_stack[row:row + DH, slot].rearrange("p h n -> p (h n)"),
                                     q_scratch[b][i * DH:(i + 1) * DH, cols]).then_inc(stack_loaded[slot], 16)
                sp.dma_start(brow[:, slot].rearrange("p h n -> p (h n)"),
                             bucket_scratch[b:b + 1, cols].broadcast_to([P, 4 * SEQ])
                             if isinstance(b, int) else
                             bucket_scratch[bass.ds(b, 1), cols].broadcast_to([P, 4 * SEQ])
                             ).then_inc(stack_loaded[slot], 16)

            def iteration(i, project, attend, feed):
                p, b, f = i + 1, i, i - 1
                if attend and project:
                    sp.wait_ge(xn_done, p)
                    apart(sp)
                    sp.dma_start(x_in[:], x_view[p]).then_inc(x_loaded, 16)
                if attend:
                    if feed:
                        sp.wait_ge(y1_done, f + 1)
                        apart(sp)
                    sp.dma_start(x_res[:], x_view[b]).then_inc(x_res_loaded, 16)
                    for quad in (2, 3):
                        sp.wait_ge(logits_done, b * TILES + (quad - 1) * QT)
                        apart(sp)
                        load_stacks(b, quad)
                if project:
                    sp.wait_ge(q_part_steps, 4 * (p + 1))
                    apart(sp)
                    sp.wait_ge(brow_done, p + 1)
                    apart(sp)
                    for c in range(PARTS):
                        sp.dma_start(q_scratch[p][c * DH:(c + 1) * DH, :].rearrange("d (h n) -> (d h) n", h=H),
                                     q_parts[:, c, :]).then_inc(scratch_written, 16)
                    sp.dma_start(bucket_scratch[p].rearrange("(h n) -> h n", h=H), brow16[:]).then_inc(scratch_written, 16)
                    sp.wait_ge(scratch_written, 4 * 16 * (p + 1))
                    apart(sp)
                    if not attend:
                        sp.wait_ge(stacks_clear, 2)
                        apart(sp)
                    for quad in (0, 1):
                        if attend:
                            if quad == 1 and feed:
                                sp.wait_ge(y2_done, f + 1)
                                apart(sp)
                                sp.dma_start(out_view[f], y2[:]).then_inc(out_stored, 16)
                            sp.wait_ge(logits_done, b * TILES + (quad + 3) * QT)
                            apart(sp)
                        load_stacks(p, quad)
                    if feed:
                        sp.wait_ge(out_stored, 16 * (f + 1))
                        apart(sp)
                elif feed:
                    sp.wait_ge(y2_done, f + 1)
                    apart(sp)
                    sp.dma_start(out_view[f], y2[:]).then_inc(out_stored, 16)

            stages(sp, iteration)
            sp.wait_ge(out_stored, 16 * BATCH)

        @block.tensor
        def _(pe):
            pe.wait_ge(weights_in, 16 * WEIGHT_DMAS)
            pe.wait_ge(consts_made, 4)

            def scores(b, k):
                h, t = divmod(k, ST)
                quad, hh = divmod(h, 4)
                if k % QT == 0:
                    pe.wait_ge(stack_loaded[quad % 2], 16 * 13 * (2 * b + quad // 2 + 1))
                if begun(b) or k >= 2:
                    pe.wait_ge(logits_done, b * TILES + k - 1)
                nc.tensor.matmul(s_bank[k % 2][:], stat_stack[:, quad % 2, hh, t * P:(t + 1) * P],
                                 mov_stack[:, quad % 2, hh, :], start=True, stop=True).then_inc(scores_psum, 1)

            def transpose_tile(b, k):
                pe.wait_ge(below_max_done, b * TILES + k + 1)
                if begun(b) or k >= 2:
                    pe.wait_ge(probs_done, b * TILES + k - 1)
                for j in range(ST):
                    last = nc.tensor.transpose(t_bank[k % 2][:, j * P:(j + 1) * P],
                                               below_max[:, k % 4, j * P:(j + 1) * P], ident[:])
                last.then_inc(transposed_psum, 1)

            def weigh_values(b, quad):
                if quad == 0:
                    pe.wait_ge(v_pad_done, b + 1)
                pe.wait_ge(probs_done, b * TILES + (quad + 1) * QT)
                if begun(b) or quad:
                    pe.wait_ge(oT_done, b * QUADS + quad)
                for j in range(ST):
                    for hh in range(4):
                        last = nc.tensor.matmul(pv_bank[hh * VW:(hh + 1) * VW, :], v_pad[:, j, quad * 4 + hh, :],
                                                probs[:, quad % 2, hh, j, :], start=(j == 0), stop=(j == ST - 1))
                last.then_inc(pv_psum, 1)

            def transpose_output(b, quad, project):
                pe.wait_ge(oT_done, b * QUADS + quad + 1)
                if quad == 0 and project:
                    pe.wait_ge(brow_done, b + 2)
                else:
                    pe.wait_ge(att_done, b * QUADS + quad)
                for t in range(ST):
                    last = nc.tensor.transpose(aux_bank[:, t * P:(t + 1) * P], oT[:, t * P:(t + 1) * P], ident[:])
                last.then_inc(o_psum, 1)

            def project_step(p, k):
                if k == 6:
                    pe.wait_ge(xn_done, p + 1)
                    if begun(p - 1):
                        pe.wait_ge(att_done, (p - 1) * QUADS)
                    for t in range(ST):
                        last = nc.tensor.transpose(aux_bank[:, t * P:(t + 1) * P], xn[:, t, :], ident[:])
                    last.then_inc(xnT_psum, 1)
                if k == 9:
                    pe.wait_ge(xnT_done, p + 1)
                    nc.tensor.matmul(aux_bank[:], wq_sb[:], xnT[:], start=True, stop=True).then_inc(q_psum, 1)
                if k == 12:
                    pe.wait_ge(q_done, p + 1)
                    for t in range(ST):
                        last = nc.tensor.matmul(aux_bank[:, t * P:(t + 1) * P], xnT[:, t * P:(t + 1) * P], wv_sb[:],
                                                start=True, stop=True)
                    last.then_inc(v_psum, 1)
                if k == 15:
                    pe.wait_ge(v_next_done, p + 1)
                    for t in range(ST):
                        last = nc.tensor.matmul(aux_bank[:, t * NH * H:(t + 1) * NH * H], qT[:, t * P:(t + 1) * P],
                                                hyper_sb[:], start=True, stop=True)
                    last.then_inc(proj_psum, 1)
                if k == 20:
                    pe.wait_ge(bcol_next_done, p + 1)
                    for t in range(ST):
                        last = nc.tensor.transpose(aux_bank[0:H, t * P:(t + 1) * P], bcol_next[:, t, :], ident[:])
                    last.then_inc(brow_psum, 1)

            def hidden(w, hin, j, k, done):
                last = nc.tensor.matmul(f_bank[j % 2][:], w[:, k, j * P:(j + 1) * P], hin[:, k, :],
                                        start=(k == 0), stop=(k == HT - 1))
                if k == HT - 1:
                    last.then_inc(done, 1)

            def feed_step(f, k):
                if k == 10:
                    pe.wait_ge(yn_done, f + 1)
                    for t in range(ST):
                        last = nc.tensor.transpose(f_bank[0][:, t * P:(t + 1) * P], yn[:, t, :], ident[:])
                    last.then_inc(ynT_psum, 1)
                for pair in range(2):
                    if k == 12 + 4 * pair:
                        pe.wait_ge(ynT_done, f + 1)
                        if pair:
                            pe.wait_ge(h0_done, f * HT + 2 * pair)
                        for j in (0, 1):
                            last = nc.tensor.matmul(f_bank[j][:], w1_sb[:, (2 * pair + j) * P:(2 * pair + j + 1) * P],
                                                    ynT[:], start=True, stop=True)
                        last.then_inc(w1_psum, 1)
                    if k == 14 + 4 * pair:
                        pe.wait_ge(gate_done, 2 * f + pair + 1)
                        for j in (0, 1):
                            last = nc.tensor.matmul(f_bank[j][:], w2_sb[:, (2 * pair + j) * P:(2 * pair + j + 1) * P],
                                                    ynT[:], start=True, stop=True)
                        last.then_inc(w2_psum, 1)
                for first, w, hin, before, count, done in (
                    (20, h1_sb, hid_a, h0_done, 4, h1_psum), (28, h1_sb, hid_a, h1_done, 2, h1_psum),
                    (36, h2_sb, hid_b, h1_done, 4, h2_psum), (44, h2_sb, hid_b, h2_done, 2, h2_psum),
                ):
                    if first <= k < first + 7:
                        if k == first:
                            pe.wait_ge(before, f * HT + count)
                        for n in ((0, 1) if k == first else (k - first + 1,)):
                            hidden(w, hin, 2 * (count == 2) + n // HT, n % HT, done)
                if 53 <= k < 53 + ST:
                    t = k - 53
                    if t == 0:
                        pe.wait_ge(h2_done, f * HT + 4)
                    for j in range(HT):
                        last = nc.tensor.matmul(f_bank[0][:, t * P:(t + 1) * P], hid_a[:, j, t * P:(t + 1) * P],
                                                w3_sb[:, j, :], start=(j == 0), stop=(j == HT - 1))
                    if t == ST - 1:
                        last.then_inc(w3_psum, 1)

            def iteration(i, project, attend, feed):
                for k in range(TILES):
                    if attend:
                        scores(i, k)
                        if k >= T_LAG:
                            transpose_tile(i, k - T_LAG)
                        if k >= QT and k % QT == 5:
                            weigh_values(i, k // QT - 1)
                        if k >= QT and k % QT == 8:
                            transpose_output(i, k // QT - 1, project)
                    if project:
                        project_step(i + 1, k)
                    if feed:
                        feed_step(i - 1, k)
                if attend:
                    for k in range(TILES - T_LAG, TILES):
                        transpose_tile(i, k)
                    weigh_values(i, QUADS - 1)
                    transpose_output(i, QUADS - 1, project)

            stages(pe, iteration)

        @block.vector
        def _(dve):
            for n in range(NH):
                last = nc.vector.memset(pow2_sb[:, n, :], float(2 ** n))
            last.then_inc(consts_made, 1)
            dve.wait_ge(weights_in, 16 * WEIGHT_DMAS)
            dve.wait_ge(consts_made, 4)

            def coefficients(b, k):
                h, t = divmod(k, ST)
                nc.vector.tensor_scalar(coeff[:, k % 3, :], brow[:, h // 4 % 2, h % 4, :], bcol[:, t, h:h + 1],
                                        float(BUCKETS - 2), ALU.is_equal, ALU.add).then_inc(coeff_done, 1)

            def attend_tile(b, k):
                dve.wait_ge(scores_psum, b * TILES + k + 1)
                dve.wait_ge(coeff_done, b * TILES + k + 1)
                if k + 1 < TILES:
                    if (k + 1) % QT == 0:
                        quad = (k + 1) // QT
                        dve.wait_ge(stack_loaded[quad % 2], 16 * 13 * (2 * b + quad // 2 + 1))
                    coefficients(b, k + 1)
                else:
                    nc.vector.memset(rden[:, 0, 0:1], 1.0)
                nc.vector.tensor_tensor_reduce(
                    out=logits[:, k % 4, :], in0=s_bank[k % 2][:], in1=coeff[:, k % 3, :], scale=float(E) ** -0.5,
                    scalar=-3.0e38, op0=ALU.mult, op1=ALU.max, accum_out=rowmax[:, k:k + 1]).then_inc(logits_done, 1)

            def moments(src, stats, mv, stats_done, mv_done, step, n):
                if step == 0:
                    for t in range(ST):
                        last = nc.vector.bn_stats(stats[:, t, :], src[:, t, :])
                    last.then_inc(stats_done, 1)
                else:
                    dve.wait_ge(stats_done, n)
                    apart(dve)
                    for t in range(ST):
                        last = nc.vector.bn_aggr(mv[:, t, :], stats[:, t, :])
                    last.then_inc(mv_done, 1)

            def normalise(dst, src, mv, rstd, done):
                for t in range(ST):
                    last = nc.vector.tensor_scalar(dst[:, t, :], src[:, t, :], mv[:, t, 0:1], rstd[:, t:t + 1],
                                                   ALU.subtract, ALU.mult)
                last.then_inc(done, 1)

            def output_step(b, quad, step):
                o4 = aux_bank[:].rearrange("p (t h w) -> p t h w", t=ST, w=VW)
                if step == 0:
                    dve.wait_ge(o_psum, b * QUADS + quad + 1)
                    nc.vector.reciprocal(rden[:].unsqueeze(3), o4[:, :, :, DH:DH + 1]).then_inc(rden_done, 1)
                else:
                    dve.wait_ge(rden_done, b * QUADS + quad + 1)
                    nc.vector.tensor_tensor(
                        att[:, :, quad * 4 * DH:(quad + 1) * 4 * DH].rearrange("p t (h d) -> p t h d", d=DH),
                        o4[:, :, :, 0:DH], rden[:].unsqueeze(3).broadcast_to([P, ST, 4, DH]),
                        ALU.mult).then_inc(att_done, 1)

            def project_step(p, k):
                if k == 1:
                    dve.wait_ge(x_loaded, 16 * (p + 1))
                    moments(x_in, x_stats, x_mv, x_stats_done, x_mv_done, 0, p + 1)
                if k == 2:
                    moments(x_in, x_stats, x_mv, x_stats_done, x_mv_done, 1, p + 1)
                if k == 4:
                    dve.wait_ge(x_rstd_done, p + 1)
                    normalise(xn, x_in, x_mv, x_rstd, xn_done)
                if k == 13:
                    dve.wait_ge(v_psum, p + 1)
                    nc.vector.tensor_tensor(v_next[:].rearrange("p t h d -> p t (h d)"),
                                            aux_bank[:].rearrange("p (t e) -> p t e", t=ST),
                                            bv_sb[:].unsqueeze(1).broadcast_to([P, ST, E]), ALU.add).then_inc(v_next_done, 1)
                if k == 16:
                    dve.wait_ge(proj_psum, p + 1)
                    nc.vector.tensor_tensor(proj[:].rearrange("p t n h -> p t (n h)"),
                                            aux_bank[:, 0:ST * NH * H].rearrange("p (t e) -> p t e", t=ST),
                                            hbias_sb[:].rearrange("p n h -> p (n h)").unsqueeze(1).broadcast_to([P, ST, NH * H]),
                                            ALU.add).then_inc(proj_done, 1)
                if k == 17:
                    dve.wait_ge(proj_done, p + 1)
                    nc.vector.scalar_tensor_tensor(out=bits[:].rearrange("p t n h -> p t (n h)"),
                                                   in0=proj[:].rearrange("p t n h -> p t (n h)"), scalar=0.0,
                                                   in1=pow2_sb[:].rearrange("p n h -> p (n h)").unsqueeze(1).broadcast_to([P, ST, NH * H]),
                                                   op0=ALU.is_ge, op1=ALU.mult).then_inc(bits_done, 1)
                if k == 18:
                    dve.wait_ge(bits_done, p + 1)
                    nc.vector.reduce_sum(bcol_next[:], bits[:].rearrange("p t n h -> p t h n"), AXIS_X).then_inc(bcol_next_done, 1)

            def feed_step(f, k):
                if k == 0:
                    dve.wait_ge(att_done, QUADS * (f + 1))
                    moments(att, att_stats, att_mv, att_stats_done, att_mv_done, 0, 3 * f + 1)
                if k == 1:
                    moments(att, att_stats, att_mv, att_stats_done, att_mv_done, 1, 3 * f + 1)
                if k == 3:
                    dve.wait_ge(att_rstd_done, 3 * f + 1)
                    normalise(normed, att, att_mv, att_rstd, normed_done)
                if k == 5:
                    dve.wait_ge(y1_done, f + 1)
                    moments(y1, att_stats, att_mv, att_stats_done, att_mv_done, 0, 3 * f + 2)
                if k == 6:
                    moments(y1, att_stats, att_mv, att_stats_done, att_mv_done, 1, 3 * f + 2)
                if k == 8:
                    dve.wait_ge(att_rstd_done, 3 * f + 2)
                    normalise(yn, y1, att_mv, att_rstd, yn_done)
                for pair in range(2):
                    if k == 15 + 4 * pair:
                        dve.wait_ge(w2_psum, 2 * f + pair + 1)
                        for j in (0, 1):
                            nc.vector.scalar_tensor_tensor(
                                out=hid_a[:, 2 * pair + j, :], in0=f_bank[j][:],
                                scalar=scales_sb[:, 1, 2 * pair + j:2 * pair + j + 1],
                                in1=gate[:, j, :], op0=ALU.mult, op1=ALU.mult).then_inc(h0_done, 1)
                if k == 57:
                    dve.wait_ge(w3_psum, f + 1)
                    nc.vector.tensor_tensor(ffn[:], f_bank[0][:].rearrange("p (t e) -> p t e", t=ST),
                                            w3s_sb[:].unsqueeze(1).broadcast_to([P, ST, E]), ALU.mult).then_inc(ffn_done, 1)
                if k == 58:
                    dve.wait_ge(ffn_done, f + 1)
                    moments(ffn, att_stats, att_mv, att_stats_done, att_mv_done, 0, 3 * f + 3)
                if k == 59:
                    moments(ffn, att_stats, att_mv, att_stats_done, att_mv_done, 1, 3 * f + 3)
                if k == 61:
                    dve.wait_ge(att_rstd_done, 3 * f + 3)
                    normalise(normed, ffn, att_mv, att_rstd, normed_done)

            def iteration(i, project, attend, feed):
                if attend:
                    dve.wait_ge(bcol_next_done, i + 1)
                    nc.vector.tensor_copy(bcol[:], bcol_next[:]).then_inc(bcol_done, 1)
                    dve.wait_ge(stack_loaded[0], 16 * 13 * (2 * i + 1))
                    dve.wait_ge(bcol_done, i + 1)
                    coefficients(i, 0)
                for k in range(TILES):
                    if attend:
                        attend_tile(i, k)
                        if k >= QT and k % QT in (10, 11):
                            output_step(i, k // QT - 1, k % QT - 10)
                    if project:
                        project_step(i + 1, k)
                    if feed:
                        feed_step(i - 1, k)
                if attend:
                    output_step(i, QUADS - 1, 0)
                    output_step(i, QUADS - 1, 1)

            stages(dve, iteration)

        @block.gpsimd
        def _(pool):
            nc.gpsimd.memset(ident[:], 0.0).then_inc(consts_made, 1)
            nc.gpsimd.memset(minus_half[:], -0.5).then_inc(consts_made, 1)
            nc.gpsimd.memset(v_pad[:], 0.0).then_inc(stacks_clear, 1)
            nc.gpsimd.memset(stat_stack[:], 0.0).then_inc(stacks_clear, 1)
            nc.gpsimd.memset(mov_stack[:], 0.0).then_inc(stacks_clear, 1)
            pool.wait_ge(stacks_clear, 3)
            nc.gpsimd.memset(v_pad[:, :, :, DH:DH + 1], 1.0).then_inc(stacks_clear, 1)
            pool.wait_ge(consts_made, 1)
            nc.gpsimd.affine_select(out=ident[:], in_=ident[:], compare_op=ALU.not_equal, fill=1.0, base=0,
                                    pattern=[[-1, P]], channel_multiplier=1).then_inc(consts_made, 1)
            pool.wait_ge(consts_made, 4)

            def rstd(mv, var, out_, ready, var_done, done, n):
                pool.wait_ge(ready, n)
                apart(pool)
                nc.gpsimd.tensor_scalar(var[:], mv[:, :, 1], EPS, 1.0, ALU.add, ALU.mult).then_inc(var_done, 1)
                pool.wait_ge(var_done, n)
                apart(pool)
                nc.gpsimd.tensor_tensor(out_[:], var[:], minus_half[:], ALU.pow).then_inc(done, 1)

            def iteration(i, project, attend, feed):
                p, b, f = i + 1, i, i - 1
                for k in range(TILES):
                    if attend:
                        pool.wait_ge(logits_done, b * TILES + k + 1)
                        apart(pool)
                        nc.gpsimd.tensor_scalar(below_max[:, k % 4, :], logits[:, k % 4, :], -1.0, rowmax[:, k:k + 1],
                                                ALU.mult, ALU.add).then_inc(below_max_done, 1)
                    if project:
                        if k == 3:
                            rstd(x_mv, x_var, x_rstd, x_mv_done, x_var_done, x_rstd_done, p + 1)
                        if k == 11:
                            pool.wait_ge(q_done, p + 1)
                            apart(pool)
                            if attend:
                                pool.wait_ge(scratch_written, 4 * 16 * p)
                                apart(pool)
                            nc.gpsimd.tensor_copy(q_parts[:, 0, :], qT[:]).then_inc(q_part_steps, 1)
                        if k == 12:
                            pool.wait_ge(q_part_steps, 4 * p + 1)
                            apart(pool)
                            nc.gpsimd.tensor_tensor(q_rest[:, 0, :], qT[:], q_parts[:, 0, :], ALU.subtract).then_inc(q_part_steps, 1)
                        if k == 13:
                            pool.wait_ge(q_part_steps, 4 * p + 2)
                            apart(pool)
                            nc.gpsimd.tensor_copy(q_parts[:, 1, :], q_rest[:, 0, :]).then_inc(q_part_steps, 1)
                        if k == 14:
                            pool.wait_ge(q_part_steps, 4 * p + 3)
                            apart(pool)
                            nc.gpsimd.tensor_tensor(q_parts[:, 2, :], q_rest[:, 0, :], q_parts[:, 1, :],
                                                    ALU.subtract).then_inc(q_part_steps, 1)
                    if feed:
                        for n, at in enumerate((2, 7, 60)):
                            if k == at:
                                rstd(att_mv, att_var, att_rstd, att_mv_done, att_var_done, att_rstd_done, 3 * f + n + 1)
                        if k == 4:
                            pool.wait_ge(normed_done, 2 * f + 1)
                            apart(pool)
                            pool.wait_ge(x_res_loaded, 16 * (f + 1))
                            apart(pool)
                            nc.gpsimd.tensor_tensor(y1[:], normed[:], x_res[:], ALU.add).then_inc(y1_done, 1)
                        if k == 62:
                            pool.wait_ge(normed_done, 2 * f + 2)
                            apart(pool)
                            if not project:
                                pool.wait_ge(out_stored, 16 * f)
                                apart(pool)
                            nc.gpsimd.tensor_tensor(y2[:], normed[:], y1[:], ALU.add).then_inc(y2_done, 1)

            stages(pool, iteration)

        @block.scalar
        def _(act):
            act.wait_ge(weights_in, 16 * WEIGHT_DMAS)

            def exponential(b, k):
                h, t = divmod(k, ST)
                act.wait_ge(transposed_psum, b * TILES + k + 1)
                nc.scalar.activation(probs[:, h // 4 % 2, h % 4, :, t * P:(t + 1) * P],
                                     t_bank[k % 2][:].rearrange("p (j s) -> p j s", j=ST),
                                     ACT.Exp, scale=-1.0).then_inc(probs_done, 1)

            def copy_output(b, quad):
                act.wait_ge(pv_psum, b * QUADS + quad + 1)
                if begun(b) or quad:
                    act.wait_ge(o_psum, b * QUADS + quad)
                nc.scalar.copy(oT[:], pv_bank[:]).then_inc(oT_done, 1)

            def project_step(p, k):
                if k == 7:
                    act.wait_ge(xnT_psum, p + 1)
                    nc.scalar.copy(xnT[:], aux_bank[:]).then_inc(xnT_done, 1)
                if k == 10:
                    act.wait_ge(q_psum, p + 1)
                    nc.scalar.activation(qT[:], aux_bank[:], ACT.Identity, bias=bq_sb[:]).then_inc(q_done, 1)
                if k == 21:
                    act.wait_ge(brow_psum, p + 1)
                    if begun(p):
                        act.wait_ge(scratch_written, 4 * 16 * p)
                    nc.scalar.copy(brow16[:], aux_bank[0:H, :]).then_inc(brow_done, 1)

            def gelus(f, first, psum, dst, scale, done):
                act.wait_ge(psum, f * HT + first + 2)
                for j in (first, first + 1):
                    nc.scalar.activation(dst[:, j, :], f_bank[j % 2][:], ACT.Gelu,
                                         scale=scales_sb[:, scale, j:j + 1]).then_inc(done, 1)

            def feed_step(f, k):
                if k == 11:
                    act.wait_ge(ynT_psum, f + 1)
                    nc.scalar.copy(ynT[:], f_bank[0][:]).then_inc(ynT_done, 1)
                for pair in range(2):
                    if k == 13 + 4 * pair:
                        act.wait_ge(w1_psum, 2 * f + pair + 1)
                        if pair:
                            act.wait_ge(h0_done, f * HT + 2)
                        for j in (0, 1):
                            last = nc.scalar.activation(gate[:, j, :], f_bank[j][:], ACT.Silu,
                                                        scale=scales_sb[:, 0, 2 * pair + j:2 * pair + j + 1])
                        last.then_inc(gate_done, 1)
                if k in (27, 35):
                    gelus(f, 0 if k == 27 else 2, h1_psum, hid_b, 2, h1_done)
                if k in (43, 51):
                    gelus(f, 0 if k == 43 else 2, h2_psum, hid_a, 3, h2_done)

            def iteration(i, project, attend, feed):
                if attend:
                    act.wait_ge(v_next_done, i + 1)
                    if begun(i):
                        act.wait_ge(pv_psum, i * QUADS)
                    act.wait_ge(stacks_clear, 4)
                    nc.scalar.copy(v_pad[:, :, :, 0:DH], v_next[:]).then_inc(v_pad_done, 1)
                for k in range(TILES):
                    if attend:
                        if k >= X_LAG:
                            exponential(i, k - X_LAG)
                        if k >= QT and k % QT == 6:
                            copy_output(i, k // QT - 1)
                    if project:
                        project_step(i + 1, k)
                    if feed:
                        feed_step(i - 1, k)
                if attend:
                    for k in range(TILES - X_LAG, TILES):
                        exponential(i, k)
                    copy_output(i, QUADS - 1)

            stages(act, iteration)


def kernel(L0_attn_x, L0_attn_Wq, L0_attn_bq, L0_attn_Wv, L0_attn_bv, L0_attn_hyperplanes, L0_ffn_w1_w, L0_ffn_w1_s,
           L0_ffn_w2_w, L0_ffn_w2_s, L0_ffn_h1_w, L0_ffn_h1_s, L0_ffn_h2_w, L0_ffn_h2_s, L0_ffn_w3_w, L0_ffn_w3_s):
    import numpy as np
    from concourse import bacc
    from concourse.bass_utils import run_bass_kernel_spmd

    flat = np.ascontiguousarray
    wq = flat(np.asarray(L0_attn_Wq).reshape(H, DH, E).transpose(1, 0, 2).reshape(E, E).T)
    bq = flat(np.asarray(L0_attn_bq).reshape(H, DH).T.reshape(E))
    planes = np.asarray(L0_attn_hyperplanes)
    blocks = np.zeros((DH, H, NH, H), planes.dtype)
    bias = np.zeros((NH, H), planes.dtype)
    for h in range(H):
        blocks[:, h, :, h] = planes[:DH]
        bias[:, h] = planes[DH]
    scales = np.stack([np.asarray(s).reshape(HT, P) for s in (L0_ffn_w1_s, L0_ffn_w2_s, L0_ffn_h1_s, L0_ffn_h2_s)])
    scales = scales.transpose(2, 0, 1)
    arrays = {
        "x": flat(L0_attn_x), "wqT": wq, "bq": bq, "wvT": flat(np.asarray(L0_attn_Wv).T), "bv": flat(L0_attn_bv),
        "hyper_blocks": blocks.reshape(E, NH * H), "hyper_bias": bias.reshape(NH * H),
        "w1T": flat(np.asarray(L0_ffn_w1_w).T), "w2T": flat(np.asarray(L0_ffn_w2_w).T),
        "h1T": flat(np.asarray(L0_ffn_h1_w).T), "h2T": flat(np.asarray(L0_ffn_h2_w).T), "scales": flat(scales),
        "w3T": flat(np.asarray(L0_ffn_w3_w).T), "w3_s": flat(L0_ffn_w3_s),
    }
    nc = bacc.Bacc("TRN2", target_bir_lowering=False, num_devices=1)
    args = {n: nc.dram_tensor(f"in_{n}", a.shape, mybir.dt.from_np(a.dtype), kind="ExternalInput").ap()
            for n, a in arrays.items()}
    out = nc.dram_tensor("out", (BATCH, SEQ, E), FP32, kind="ExternalOutput").ap()
    sandwich_kernel(nc, **args, out=out)
    result = run_bass_kernel_spmd(nc, [{f"in_{n}": a for n, a in arrays.items()}], core_ids=[0])
    return result.results[0]["out"]
```

```python
from contextlib import ExitStack

import concourse.bass as bass
from concourse import mybir

FP32 = mybir.dt.float32
BF16 = mybir.dt.bfloat16
ALU = mybir.AluOpType
ACT = mybir.ActivationFunctionType
AXIS_X = mybir.AxisListType.X

P = 128
E = 128
H = 16
DH = E // H
NH = 6
BUCKETS = 2 ** NH
SEQ = 512
BATCH = 16
HID = 512
ST = SEQ // P
HT = HID // P
QUADS = H // 4
TILES = H * ST
QT = 4 * ST
PARTS = 3
KROWS = PARTS * PARTS * DH
VW = 32
EPS = 1e-5
MAX_LAG = 5
SUB_LAG = 7
EXP_LAG = 9
RING = 16


def sandwich_kernel(nc, x, wqT, bq, wvT, bv, hyper_blocks, hyper_bias, w1T, w2T, h1T, h2T, scales, w3T, w3_s, out):
    ctx = ExitStack()
    with ctx:
        def sb(name, shape, dt=FP32):
            return ctx.enter_context(nc.sbuf_tensor(name, shape, dt))

        def bank(name):
            return ctx.enter_context(nc.psum_tensor(name, [P, SEQ], FP32))

        def sem(name):
            return ctx.enter_context(nc.semaphore(name))

        q_scratch = nc.dram_tensor("q_scratch", [BATCH, PARTS * DH, H * SEQ], BF16, kind="Internal").ap()
        bucket_scratch = nc.dram_tensor("bucket_scratch", [BATCH, H * SEQ], BF16, kind="Internal").ap()

        wq_sb = sb("wq_sb", [P, E])
        wv_sb = sb("wv_sb", [P, E])
        bq_sb = sb("bq_sb", [P, 1])
        bv_sb = sb("bv_sb", [P, E])
        hyper_sb = sb("hyper_sb", [P, NH * H])
        hbias_sb = sb("hbias_sb", [P, NH, H])
        pow2_sb = sb("pow2_sb", [P, NH, H])
        w1_sb = sb("w1_sb", [P, HID])
        w2_sb = sb("w2_sb", [P, HID])
        h1_sb = sb("h1_sb", [P, HT, HID])
        h2_sb = sb("h2_sb", [P, HT, HID])
        w3_sb = sb("w3_sb", [P, HT, E])
        scales_sb = sb("scales_sb", [P, 4, HT])
        w3s_sb = sb("w3s_sb", [P, E])
        ident = sb("ident", [P, P])
        minus_half = sb("minus_half", [P, ST])

        x_in = sb("x_in", [P, ST, E])
        x_stats = sb("x_stats", [P, ST, 6])
        x_mv = sb("x_mv", [P, ST, 2])
        x_var = sb("x_var", [P, ST])
        x_rstd = sb("x_rstd", [P, ST])
        xnT = sb("xnT", [P, SEQ])
        qT = sb("qT", [P, SEQ])
        q_rest = xnT
        q_parts = sb("q_parts", [P, PARTS, SEQ], BF16)
        v_next = sb("v_next", [P, ST, H, DH])
        proj = sb("proj", [P, ST, NH, H])
        bcol_next = sb("bcol_next", [P, ST, H])
        brow16 = sb("brow16", [H, SEQ], BF16)

        stat_stack = sb("stat_stack", [P, 2, 4, SEQ], BF16)
        mov_stack = sb("mov_stack", [P, 2, 4, SEQ], BF16)
        brow = sb("brow", [P, 2, 4, SEQ], BF16)
        bcol = sb("bcol", [P, ST, H])
        coeff = sb("coeff", [P, 3, SEQ], BF16)
        logits = sb("logits", [P, RING, SEQ])
        rowmax = sb("rowmax", [P, TILES])
        max_row = sb("max_row", [P, 2, SEQ])
        probs = sb("probs", [P, 2, 4, ST, SEQ])
        v_pad = sb("v_pad", [P, ST, H, VW])
        oT = sb("oT", [P, SEQ])
        rden = sb("rden", [P, ST, 4])
        spare = sb("spare", [P, 1])
        att = sb("att", [P, ST, E])

        x_res = sb("x_res", [P, ST, E])
        att_stats = sb("att_stats", [P, ST, 6])
        att_mv = sb("att_mv", [P, ST, 2])
        att_var = sb("att_var", [P, ST])
        att_rstd = sb("att_rstd", [P, ST])
        y1 = sb("y1", [P, ST, E])
        y1_kept = sb("y1_kept", [P, ST, E])
        end_stats = sb("end_stats", [P, ST, 6])
        end_mv = sb("end_mv", [P, ST, 2])
        end_var = sb("end_var", [P, ST])
        end_rstd = sb("end_rstd", [P, ST])
        ynT = sb("ynT", [P, SEQ])
        hid_a = sb("hid_a", [P, HT, SEQ])
        hid_b = sb("hid_b", [P, HT, SEQ])
        ffn = sb("ffn", [P, ST, E])

        s_bank = [bank(f"s_bank{n}") for n in range(3)]
        max_bank = bank("max_bank")
        f_bank = [bank(f"f_bank{n}") for n in range(2)]
        pv_bank = bank("pv_bank")
        aux_bank = bank("aux_bank")

        weights_in = sem("weights_in")
        stacks_clear = sem("stacks_clear")
        consts_made = sem("consts_made")
        x_loaded = sem("x_loaded")
        x_stats_done = sem("x_stats_done")
        x_mv_done = sem("x_mv_done")
        x_var_done = sem("x_var_done")
        x_rstd_done = sem("x_rstd_done")
        xn_done = sem("xn_done")
        xnT_psum = sem("xnT_psum")
        xnT_done = sem("xnT_done")
        q_psum = sem("q_psum")
        q_done = sem("q_done")
        v_psum = sem("v_psum")
        v_next_done = sem("v_next_done")
        proj_psum = sem("proj_psum")
        proj_done = sem("proj_done")
        bits_done = sem("bits_done")
        bcol_next_done = sem("bcol_next_done")
        brow_psum = sem("brow_psum")
        brow_done = sem("brow_done")
        q_part_steps = sem("q_part_steps")
        scratch_written = sem("scratch_written")
        stack_loaded = [sem(f"stack_loaded{n}") for n in range(2)]
        bcol_done = sem("bcol_done")
        v_pad_done = sem("v_pad_done")
        scores_psum = sem("scores_psum")
        coeff_done = sem("coeff_done")
        logits_done = sem("logits_done")
        max_psum = sem("max_psum")
        max_row_done = sem("max_row_done")
        below_max_done = sem("below_max_done")
        probs_done = sem("probs_done")
        pv_psum = sem("pv_psum")
        oT_done = sem("oT_done")
        o_psum = sem("o_psum")
        rden_done = sem("rden_done")
        att_done = sem("att_done")
        x_res_loaded = sem("x_res_loaded")
        att_stats_done = sem("att_stats_done")
        att_mv_done = sem("att_mv_done")
        att_var_done = sem("att_var_done")
        att_rstd_done = sem("att_rstd_done")
        normed_done = sem("normed_done")
        y1_done = sem("y1_done")
        y1_kept_done = sem("y1_kept_done")
        end_stats_done = sem("end_stats_done")
        end_mv_done = sem("end_mv_done")
        end_var_done = sem("end_var_done")
        end_rstd_done = sem("end_rstd_done")
        end_normed_done = sem("end_normed_done")
        yn_done = sem("yn_done")
        ynT_psum = sem("ynT_psum")
        ynT_done = sem("ynT_done")
        w1_psum = sem("w1_psum")
        gate_done = sem("gate_done")
        w2_psum = sem("w2_psum")
        h0_done = sem("h0_done")
        h1_psum = sem("h1_psum")
        h1_done = sem("h1_done")
        h2_psum = sem("h2_psum")
        h2_done = sem("h2_done")
        w3_psum = sem("w3_psum")
        ffn_done = sem("ffn_done")
        y2_done = sem("y2_done")
        out_stored = sem("out_stored")
        waited = sem("waited")

        WEIGHT_DMAS = 13
        x_view = x.rearrange("b (s p) e -> b p s e", p=P)
        out_view = out.rearrange("b (s p) e -> b p s e", p=P)

        def apart(eng):
            eng.sem_inc(waited, 1)

        def begun(b):
            return not isinstance(b, int) or b > 0

        def stages(eng, iteration):
            iteration(-1, project=True, attend=False, feed=False, finish=False)
            iteration(0, project=True, attend=True, feed=False, finish=False)
            iteration(1, project=True, attend=True, feed=True, finish=False)
            with eng.Fori(2, BATCH - 1) as i:
                iteration(i, project=True, attend=True, feed=True, finish=True)
            iteration(BATCH - 1, project=False, attend=True, feed=True, finish=True)
            iteration(BATCH, project=False, attend=False, feed=True, finish=True)
            iteration(BATCH + 1, project=False, attend=False, feed=False, finish=True)

        block = ctx.enter_context(nc.Block())

        @block.sync
        def _(sp):
            sp.dma_start(x_in[:], x_view[0]).then_inc(x_loaded, 16)
            for dst, src in (
                (wq_sb[:], wqT), (bq_sb[:], bq.rearrange("(p a) -> p a", a=1)),
                (wv_sb[:], wvT), (bv_sb[:], bv.rearrange("(a e) -> a e", a=1).broadcast_to([P, E])),
                (hyper_sb[:], hyper_blocks),
                (hbias_sb[:].rearrange("p n h -> p (n h)"),
                 hyper_bias.rearrange("(a e) -> a e", a=1).broadcast_to([P, NH * H])),
                (w1_sb[:], w1T), (w2_sb[:], w2T),
                (h1_sb[:], h1T.rearrange("(k p) n -> p k n", p=P)),
                (h2_sb[:], h2T.rearrange("(k p) n -> p k n", p=P)),
                (scales_sb[:], scales),
                (w3_sb[:], w3T.rearrange("(k p) n -> p k n", p=P)),
                (w3s_sb[:], w3_s.rearrange("(a e) -> a e", a=1).broadcast_to([P, E])),
            ):
                sp.dma_start(dst, src).then_inc(weights_in, 16)

            def load_stacks(b, quad):
                slot = quad % 2
                cols = slice(quad * 4 * SEQ, (quad + 1) * 4 * SEQ)
                for i in range(PARTS):
                    sp.dma_start(mov_stack[i * PARTS * DH:(i + 1) * PARTS * DH, slot].rearrange("p h n -> p (h n)"),
                                 q_scratch[b][:, cols]).then_inc(stack_loaded[slot], 16)
                    for j in range(PARTS):
                        row = (i * PARTS + j) * DH
                        sp.dma_start(stat_stack[row:row + DH, slot].rearrange("p h n -> p (h n)"),
                                     q_scratch[b][i * DH:(i + 1) * DH, cols]).then_inc(stack_loaded[slot], 16)
                sp.dma_start(brow[:, slot].rearrange("p h n -> p (h n)"),
                             bucket_scratch[b:b + 1, cols].broadcast_to([P, 4 * SEQ])
                             if isinstance(b, int) else
                             bucket_scratch[bass.ds(b, 1), cols].broadcast_to([P, 4 * SEQ])
                             ).then_inc(stack_loaded[slot], 16)

            def store_output(g):
                sp.wait_ge(y2_done, g + 1)
                apart(sp)
                sp.dma_start(out_view[g], ffn[:]).then_inc(out_stored, 16)

            def iteration(i, project, attend, feed, finish):
                p, b, f, g = i + 1, i, i - 1, i - 2
                if attend and project:
                    sp.wait_ge(xnT_psum, p)
                    apart(sp)
                    sp.dma_start(x_in[:], x_view[p]).then_inc(x_loaded, 16)
                if attend:
                    sp.wait_ge(logits_done, b * TILES + QT)
                    apart(sp)
                    load_stacks(b, 2)
                    if feed:
                        sp.wait_ge(ynT_psum, f + 1)
                        apart(sp)
                    sp.dma_start(x_res[:], x_view[b]).then_inc(x_res_loaded, 16)
                    sp.wait_ge(logits_done, b * TILES + 2 * QT)
                    apart(sp)
                    load_stacks(b, 3)
                if finish:
                    store_output(g)
                if project:
                    sp.wait_ge(q_part_steps, 4 * (p + 1))
                    apart(sp)
                    sp.wait_ge(brow_done, p + 1)
                    apart(sp)
                    for c in range(PARTS):
                        sp.dma_start(q_scratch[p][c * DH:(c + 1) * DH, :].rearrange("d (h n) -> (d h) n", h=H),
                                     q_parts[:, c, :]).then_inc(scratch_written, 16)
                    sp.dma_start(bucket_scratch[p].rearrange("(h n) -> h n", h=H), brow16[:]).then_inc(scratch_written, 16)
                    sp.wait_ge(scratch_written, 4 * 16 * (p + 1))
                    apart(sp)
                    if not attend:
                        sp.wait_ge(stacks_clear, 3)
                    for quad in (0, 1):
                        if attend:
                            sp.wait_ge(logits_done, b * TILES + (quad + 3) * QT)
                            apart(sp)
                        load_stacks(p, quad)
                if finish and project:
                    sp.wait_ge(out_stored, 16 * (g + 1))
                    apart(sp)

            stages(sp, iteration)
            sp.wait_ge(out_stored, 16 * BATCH)

        @block.tensor
        def _(pe):
            pe.wait_ge(weights_in, 16 * WEIGHT_DMAS)
            pe.wait_ge(consts_made, 4)

            def scores(b, k):
                h, t = divmod(k, ST)
                quad, hh = divmod(h, 4)
                if k % QT == 0:
                    pe.wait_ge(stack_loaded[quad % 2], 16 * 13 * (2 * b + quad // 2 + 1))
                if begun(b) or k >= 3:
                    pe.wait_ge(logits_done, b * TILES + (k - 2 if k >= 3 else (0, -2, -1)[k]))
                nc.tensor.matmul(s_bank[k % 3][:], stat_stack[:, quad % 2, hh, t * P:(t + 1) * P],
                                 mov_stack[:, quad % 2, hh, :], start=True, stop=True).then_inc(scores_psum, 1)

            def spread_maxima(b, h):
                pe.wait_ge(logits_done, b * TILES + (h + 1) * ST)
                if begun(b) or h:
                    pe.wait_ge(max_row_done, b * H + h)
                for t in range(ST):
                    last = nc.tensor.transpose(max_bank[:, t * P:(t + 1) * P],
                                               rowmax[:, h * ST + t:h * ST + t + 1].broadcast_to([P, P]), ident[:])
                last.then_inc(max_psum, 1)

            def weigh_values(b, quad):
                if quad == 0:
                    pe.wait_ge(v_pad_done, b + 1)
                pe.wait_ge(probs_done, b * (TILES // 2) + (quad + 1) * QT // 2)
                if begun(b) or quad:
                    pe.wait_ge(oT_done, b * QUADS + quad)
                for j in range(ST):
                    for hh in range(4):
                        last = nc.tensor.matmul(pv_bank[hh * VW:(hh + 1) * VW, :], v_pad[:, j, quad * 4 + hh, :],
                                                probs[:, quad % 2, hh, j, :], start=(j == 0), stop=(j == ST - 1))
                last.then_inc(pv_psum, 1)

            def transpose_output(b, quad, project):
                pe.wait_ge(oT_done, b * QUADS + quad + 1)
                if quad == 0 and project:
                    pe.wait_ge(proj_done, b + 2)
                elif quad == 1 and project:
                    pe.wait_ge(brow_done, b + 2)
                elif begun(b) or quad:
                    pe.wait_ge(att_done, b * QUADS + quad)
                for t in range(ST):
                    last = nc.tensor.transpose(aux_bank[:, t * P:(t + 1) * P], oT[:, t * P:(t + 1) * P], ident[:])
                last.then_inc(o_psum, 1)

            def project_step(p, k, attend):
                if k == 17:
                    pe.wait_ge(xn_done, p + 1)
                    if begun(p - 1):
                        pe.wait_ge(att_done, (p - 1) * QUADS)
                    for t in range(ST):
                        last = nc.tensor.transpose(aux_bank[:, t * P:(t + 1) * P], x_in[:, t, :], ident[:])
                    last.then_inc(xnT_psum, 1)
                if k == 20:
                    pe.wait_ge(xnT_done, p + 1)
                    nc.tensor.matmul(aux_bank[:], wq_sb[:], xnT[:], start=True, stop=True).then_inc(q_psum, 1)
                if k == 22:
                    pe.wait_ge(q_done, p + 1)
                    for t in range(ST):
                        last = nc.tensor.matmul(aux_bank[:, t * P:(t + 1) * P], xnT[:, t * P:(t + 1) * P], wv_sb[:],
                                                start=True, stop=True)
                    last.then_inc(v_psum, 1)
                if k == 24:
                    pe.wait_ge(v_next_done, p + 1)
                    for t in range(ST):
                        last = nc.tensor.matmul(aux_bank[:, t * NH * H:(t + 1) * NH * H], qT[:, t * P:(t + 1) * P],
                                                hyper_sb[:], start=True, stop=True)
                    last.then_inc(proj_psum, 1)
                if k == 33:
                    pe.wait_ge(bcol_next_done, p + 1)
                    if attend:
                        pe.wait_ge(att_done, (p - 1) * QUADS + 1)
                    for t in range(ST):
                        last = nc.tensor.transpose(aux_bank[0:H, t * P:(t + 1) * P], bcol_next[:, t, :], ident[:])
                    last.then_inc(brow_psum, 1)

            def hidden(w, hin, j, k, done):
                last = nc.tensor.matmul(f_bank[j % 2][:], w[:, k, j * P:(j + 1) * P], hin[:, k, :],
                                        start=(k == 0), stop=(k == HT - 1))
                if k == HT - 1:
                    last.then_inc(done, 1)

            def feed_step(f, k, finish):
                if k == 29:
                    pe.wait_ge(yn_done, f + 1)
                    if finish:
                        pe.wait_ge(ffn_done, f)
                    for t in range(ST):
                        last = nc.tensor.transpose(f_bank[0][:, t * P:(t + 1) * P], x_res[:, t, :], ident[:])
                    last.then_inc(ynT_psum, 1)
                for pair in range(2):
                    if k == 31 + 5 * pair:
                        pe.wait_ge(ynT_done, f + 1)
                        if pair:
                            pe.wait_ge(h0_done, f * HT + 2)
                        for j in (0, 1):
                            last = nc.tensor.matmul(f_bank[j][:], w1_sb[:, (2 * pair + j) * P:(2 * pair + j + 1) * P],
                                                    ynT[:], start=True, stop=True)
                        last.then_inc(w1_psum, 1)
                    if k == 34 + 5 * pair:
                        pe.wait_ge(gate_done, 2 * f + pair + 1)
                        for j in (0, 1):
                            last = nc.tensor.matmul(f_bank[j][:], w2_sb[:, (2 * pair + j) * P:(2 * pair + j + 1) * P],
                                                    ynT[:], start=True, stop=True)
                        last.then_inc(w2_psum, 1)
                if k == 41:
                    pe.wait_ge(h0_done, f * HT + 4)
                if k == 52:
                    pe.wait_ge(h1_done, f * HT + 2)
                if 41 <= k < 49 or 52 <= k < 60:
                    n = k - 41 if k < 52 else k - 44
                    hidden(h1_sb, hid_a, n // HT, n % HT, h1_psum)

            def finish_step(g, k):
                if k == 0:
                    pe.wait_ge(h1_done, g * HT + 4)
                if k == 11:
                    pe.wait_ge(h2_done, g * HT + 2)
                if 0 <= k < 8 or 11 <= k < 19:
                    n = k if k < 11 else k - 3
                    hidden(h2_sb, hid_b, n // HT, n % HT, h2_psum)
                if 22 <= k < 22 + ST:
                    t = k - 22
                    if t == 0:
                        pe.wait_ge(h2_done, g * HT + 4)
                    for j in range(HT):
                        last = nc.tensor.matmul(f_bank[0][:, t * P:(t + 1) * P], hid_a[:, j, t * P:(t + 1) * P],
                                                w3_sb[:, j, :], start=(j == 0), stop=(j == HT - 1))
                    if t == ST - 1:
                        last.then_inc(w3_psum, 1)

            def iteration(i, project, attend, feed, finish):
                for k in range(TILES):
                    if attend:
                        scores(i, k)
                    if k % ST == MAX_LAG % ST:
                        if k >= MAX_LAG and attend:
                            spread_maxima(i, (k - MAX_LAG) // ST)
                        if k < MAX_LAG and feed:
                            spread_maxima(i - 1, H - 1)
                    if k % QT == 9:
                        if k >= QT and attend:
                            weigh_values(i, k // QT - 1)
                        if k < QT and feed:
                            weigh_values(i - 1, QUADS - 1)
                    if k % QT == 12:
                        if k >= QT and attend:
                            transpose_output(i, k // QT - 1, project)
                        if k < QT and feed:
                            transpose_output(i - 1, QUADS - 1, project)
                    if project:
                        project_step(i + 1, k, attend)
                    if finish:
                        finish_step(i - 2, k)
                    if feed:
                        feed_step(i - 1, k, finish)

            stages(pe, iteration)

        @block.vector
        def _(dve):
            for n in range(NH):
                last = nc.vector.memset(pow2_sb[:, n, :], float(2 ** n))
            last.then_inc(consts_made, 1)
            dve.wait_ge(weights_in, 16 * WEIGHT_DMAS)
            dve.wait_ge(consts_made, 4)

            def coefficients(b, k):
                h, t = divmod(k, ST)
                nc.vector.tensor_scalar(coeff[:, k % 3, :], brow[:, h // 4 % 2, h % 4, :], bcol[:, t, h:h + 1],
                                        float(BUCKETS - 2), ALU.is_equal, ALU.add).then_inc(coeff_done, 1)

            def attend_tile(b, k):
                dve.wait_ge(scores_psum, b * TILES + k + 1)
                dve.wait_ge(coeff_done, b * TILES + k + 1)
                if k % 2 == 0 and (begun(b) or k >= RING):
                    dve.wait_ge(probs_done, b * (TILES // 2) + (k - RING) // 2 + 1)
                if k + 1 < TILES:
                    if (k + 1) % QT == 0:
                        quad = (k + 1) // QT
                        dve.wait_ge(stack_loaded[quad % 2], 16 * 13 * (2 * b + quad // 2 + 1))
                    coefficients(b, k + 1)
                else:
                    nc.vector.memset(spare[:], 1.0)
                nc.vector.tensor_tensor_reduce(
                    out=logits[:, k % RING, :], in0=s_bank[k % 3][:], in1=coeff[:, k % 3, :], scale=float(E) ** -0.5,
                    scalar=-3.0e38, op0=ALU.mult, op1=ALU.max, accum_out=rowmax[:, k:k + 1]).then_inc(logits_done, 1)

            def moments(src, stats, mv, stats_done, mv_done, step, n):
                if step == 0:
                    for t in range(ST):
                        last = nc.vector.bn_stats(stats[:, t, :], src[:, t, :])
                    last.then_inc(stats_done, 1)
                else:
                    dve.wait_ge(stats_done, n)
                    apart(dve)
                    for t in range(ST):
                        last = nc.vector.bn_aggr(mv[:, t, :], stats[:, t, :])
                    last.then_inc(mv_done, 1)

            def normalise(dst, src, mv, rstd, done):
                for t in range(ST):
                    last = nc.vector.tensor_scalar(dst[:, t, :], src[:, t, :], mv[:, t, 0:1], rstd[:, t:t + 1],
                                                   ALU.subtract, ALU.mult)
                last.then_inc(done, 1)

            def output_step(b, quad, step):
                o4 = aux_bank[:].rearrange("p (t h w) -> p t h w", t=ST, w=VW)
                if step == 0:
                    dve.wait_ge(o_psum, b * QUADS + quad + 1)
                    nc.vector.reciprocal(rden[:].unsqueeze(3), o4[:, :, :, DH:DH + 1]).then_inc(rden_done, 1)
                else:
                    dve.wait_ge(rden_done, b * QUADS + quad + 1)
                    nc.vector.tensor_tensor(
                        att[:, :, quad * 4 * DH:(quad + 1) * 4 * DH].rearrange("p t (h d) -> p t h d", d=DH),
                        o4[:, :, :, 0:DH], rden[:].unsqueeze(3).broadcast_to([P, ST, 4, DH]),
                        ALU.mult).then_inc(att_done, 1)

            def project_step(p, k):
                if k == 1:
                    dve.wait_ge(x_loaded, 16 * (p + 1))
                    moments(x_in, x_stats, x_mv, x_stats_done, x_mv_done, 0, p + 1)
                if k == 2:
                    moments(x_in, x_stats, x_mv, x_stats_done, x_mv_done, 1, p + 1)
                if k == 4:
                    dve.wait_ge(x_rstd_done, p + 1)
                    normalise(x_in, x_in, x_mv, x_rstd, xn_done)
                if k == 23:
                    dve.wait_ge(v_psum, p + 1)
                    nc.vector.tensor_tensor(v_next[:].rearrange("p t h d -> p t (h d)"),
                                            aux_bank[:].rearrange("p (t e) -> p t e", t=ST),
                                            bv_sb[:].unsqueeze(1).broadcast_to([P, ST, E]), ALU.add).then_inc(v_next_done, 1)
                if k == 25:
                    dve.wait_ge(proj_psum, p + 1)
                    nc.vector.tensor_tensor(proj[:].rearrange("p t n h -> p t (n h)"),
                                            aux_bank[:, 0:ST * NH * H].rearrange("p (t e) -> p t e", t=ST),
                                            hbias_sb[:].rearrange("p n h -> p (n h)").unsqueeze(1).broadcast_to([P, ST, NH * H]),
                                            ALU.add).then_inc(proj_done, 1)
                if k == 26:
                    dve.wait_ge(proj_done, p + 1)
                    nc.vector.scalar_tensor_tensor(out=proj[:].rearrange("p t n h -> p t (n h)"),
                                                   in0=proj[:].rearrange("p t n h -> p t (n h)"), scalar=0.0,
                                                   in1=pow2_sb[:].rearrange("p n h -> p (n h)").unsqueeze(1).broadcast_to([P, ST, NH * H]),
                                                   op0=ALU.is_ge, op1=ALU.mult).then_inc(bits_done, 1)
                if k == 28:
                    dve.wait_ge(bits_done, p + 1)
                    nc.vector.reduce_sum(bcol_next[:], proj[:].rearrange("p t n h -> p t h n"), AXIS_X).then_inc(bcol_next_done, 1)
                if k == 29:
                    dve.wait_ge(q_part_steps, 4 * p + 1)
                    nc.vector.tensor_tensor(q_rest[:], qT[:], q_parts[:, 0, :], ALU.subtract).then_inc(q_part_steps, 1)
                if k == 34:
                    dve.wait_ge(q_part_steps, 4 * p + 3)
                    nc.vector.tensor_tensor(q_parts[:, 2, :], q_rest[:], q_parts[:, 1, :],
                                            ALU.subtract).then_inc(q_part_steps, 1)

            def feed_step(f, k):
                if k == 16:
                    dve.wait_ge(att_done, QUADS * (f + 1))
                    moments(att, att_stats, att_mv, att_stats_done, att_mv_done, 0, 2 * f + 1)
                if k == 17:
                    moments(att, att_stats, att_mv, att_stats_done, att_mv_done, 1, 2 * f + 1)
                if k == 19:
                    dve.wait_ge(att_rstd_done, 2 * f + 1)
                    normalise(y1, att, att_mv, att_rstd, normed_done)
                if k == 20:
                    dve.wait_ge(normed_done, f + 1)
                    dve.wait_ge(x_res_loaded, 16 * (f + 1))
                    nc.vector.tensor_tensor(y1[:], y1[:], x_res[:], ALU.add).then_inc(y1_done, 1)
                if k == 21:
                    dve.wait_ge(y1_done, f + 1)
                    moments(y1, att_stats, att_mv, att_stats_done, att_mv_done, 0, 2 * f + 2)
                if k == 22:
                    moments(y1, att_stats, att_mv, att_stats_done, att_mv_done, 1, 2 * f + 2)
                if k == 24:
                    dve.wait_ge(att_rstd_done, 2 * f + 2)
                    normalise(x_res, y1, att_mv, att_rstd, yn_done)
                for pair in range(2):
                    if k == 35 + 5 * pair:
                        dve.wait_ge(w2_psum, 2 * f + pair + 1)
                        for j in (0, 1):
                            nc.vector.scalar_tensor_tensor(
                                out=hid_a[:, 2 * pair + j, :], in0=f_bank[j][:],
                                scalar=scales_sb[:, 1, 2 * pair + j:2 * pair + j + 1],
                                in1=hid_a[:, 2 * pair + j, :], op0=ALU.mult, op1=ALU.mult).then_inc(h0_done, 1)

            def finish_step(g, k):
                if k == 16:
                    if isinstance(g, int) and g:
                        dve.wait_ge(y2_done, g)
                    nc.vector.tensor_copy(y1_kept[:], y1[:]).then_inc(y1_kept_done, 1)
                if k == 27:
                    dve.wait_ge(w3_psum, g + 1)
                    if isinstance(g, int) and g:
                        dve.wait_ge(out_stored, 16 * g)
                    nc.vector.tensor_tensor(ffn[:], f_bank[0][:].rearrange("p (t e) -> p t e", t=ST),
                                            w3s_sb[:].unsqueeze(1).broadcast_to([P, ST, E]), ALU.mult).then_inc(ffn_done, 1)
                if k == 30:
                    dve.wait_ge(ffn_done, g + 1)
                    moments(ffn, end_stats, end_mv, end_stats_done, end_mv_done, 0, g + 1)
                if k == 31:
                    moments(ffn, end_stats, end_mv, end_stats_done, end_mv_done, 1, g + 1)
                if k == 33:
                    dve.wait_ge(end_rstd_done, g + 1)
                    normalise(ffn, ffn, end_mv, end_rstd, end_normed_done)
                if k == 36:
                    dve.wait_ge(end_normed_done, g + 1)
                    dve.wait_ge(y1_kept_done, g + 1)
                    nc.vector.tensor_tensor(ffn[:], ffn[:], y1_kept[:], ALU.add).then_inc(y2_done, 1)

            def iteration(i, project, attend, feed, finish):
                if attend:
                    dve.wait_ge(bcol_next_done, i + 1)
                    nc.vector.tensor_copy(bcol[:], bcol_next[:]).then_inc(bcol_done, 1)
                    dve.wait_ge(stack_loaded[0], 16 * 13 * (2 * i + 1))
                    dve.wait_ge(bcol_done, i + 1)
                    coefficients(i, 0)
                for k in range(TILES):
                    if attend:
                        attend_tile(i, k)
                    if k % QT in (14, 15):
                        if k >= QT and attend:
                            output_step(i, k // QT - 1, k % QT - 14)
                        if k < QT and feed:
                            output_step(i - 1, QUADS - 1, k % QT - 14)
                    if project:
                        project_step(i + 1, k)
                    if finish:
                        finish_step(i - 2, k)
                    if feed:
                        feed_step(i - 1, k)

            stages(dve, iteration)

        @block.gpsimd
        def _(pool):
            nc.gpsimd.memset(ident[:], 0.0).then_inc(consts_made, 1)
            nc.gpsimd.memset(minus_half[:], -0.5).then_inc(consts_made, 1)
            nc.gpsimd.memset(v_pad[:], 0.0).then_inc(stacks_clear, 1)
            nc.gpsimd.memset(stat_stack[:], 0.0).then_inc(stacks_clear, 1)
            nc.gpsimd.memset(mov_stack[:], 0.0).then_inc(stacks_clear, 1)
            pool.wait_ge(stacks_clear, 3)
            nc.gpsimd.memset(v_pad[:, :, :, DH:DH + 1], 1.0).then_inc(stacks_clear, 1)
            pool.wait_ge(consts_made, 1)
            nc.gpsimd.affine_select(out=ident[:], in_=ident[:], compare_op=ALU.not_equal, fill=1.0, base=0,
                                    pattern=[[-1, P]], channel_multiplier=1).then_inc(consts_made, 1)
            pool.wait_ge(consts_made, 4)

            def rstd(mv, var, out_, ready, var_done, done, n):
                pool.wait_ge(ready, n)
                apart(pool)
                nc.gpsimd.tensor_scalar(var[:], mv[:, :, 1], EPS, 1.0, ALU.add, ALU.mult).then_inc(var_done, 1)
                pool.wait_ge(var_done, n)
                apart(pool)
                nc.gpsimd.tensor_tensor(out_[:], var[:], minus_half[:], ALU.pow).then_inc(done, 1)

            def subtract(b, k):
                h, t = divmod(k, ST)
                if t == 0:
                    pool.wait_ge(max_row_done, b * H + h + 1)
                pool.wait_ge(logits_done, b * TILES + k + 1)
                nc.gpsimd.tensor_tensor(logits[:, k % RING, :], max_row[:, h % 2, :], logits[:, k % RING, :],
                                        ALU.subtract).then_inc(below_max_done, 1)

            def iteration(i, project, attend, feed, finish):
                p, b, f, g = i + 1, i, i - 1, i - 2
                for k in range(TILES):
                    if k >= SUB_LAG and attend:
                        subtract(b, k - SUB_LAG)
                    if k < SUB_LAG and feed:
                        subtract(f, k - SUB_LAG + TILES)
                    if project and k == 3:
                        rstd(x_mv, x_var, x_rstd, x_mv_done, x_var_done, x_rstd_done, p + 1)
                    if finish and k == 32:
                        rstd(end_mv, end_var, end_rstd, end_mv_done, end_var_done, end_rstd_done, g + 1)
                    if feed and k == 18:
                        rstd(att_mv, att_var, att_rstd, att_mv_done, att_var_done, att_rstd_done, 2 * f + 1)
                    if feed and k == 23:
                        rstd(att_mv, att_var, att_rstd, att_mv_done, att_var_done, att_rstd_done, 2 * f + 2)

            stages(pool, iteration)

        @block.scalar
        def _(act):
            act.wait_ge(weights_in, 16 * WEIGHT_DMAS)

            def copy_maxima(b, h):
                act.wait_ge(max_psum, b * H + h + 1)
                nc.scalar.copy(max_row[:, h % 2, :], max_bank[:]).then_inc(max_row_done, 1)

            def exponential(b, k):
                h, t = divmod(k, ST)
                act.wait_ge(below_max_done, b * TILES + k + 2)
                nc.scalar.activation(probs[:, h // 4 % 2, h % 4, t:t + 2, :], logits[:, k % RING:k % RING + 2, :],
                                     ACT.Exp, scale=-1.0).then_inc(probs_done, 1)

            def copy_output(b, quad):
                act.wait_ge(pv_psum, b * QUADS + quad + 1)
                if begun(b) or quad:
                    act.wait_ge(o_psum, b * QUADS + quad)
                nc.scalar.copy(oT[:], pv_bank[:]).then_inc(oT_done, 1)

            def project_step(p, k):
                if k == 18:
                    act.wait_ge(xnT_psum, p + 1)
                    nc.scalar.copy(xnT[:], aux_bank[:]).then_inc(xnT_done, 1)
                if k == 21:
                    act.wait_ge(q_psum, p + 1)
                    nc.scalar.activation(qT[:], aux_bank[:], ACT.Identity, bias=bq_sb[:]).then_inc(q_done, 1)
                if k == 27:
                    act.wait_ge(q_done, p + 1)
                    if begun(p):
                        act.wait_ge(scratch_written, 4 * 16 * p)
                    nc.scalar.copy(q_parts[:, 0, :], qT[:]).then_inc(q_part_steps, 1)
                if k == 31:
                    act.wait_ge(q_part_steps, 4 * p + 2)
                    nc.scalar.copy(q_parts[:, 1, :], q_rest[:]).then_inc(q_part_steps, 1)
                if k == 35:
                    act.wait_ge(brow_psum, p + 1)
                    nc.scalar.copy(brow16[:], aux_bank[0:H, :]).then_inc(brow_done, 1)

            def gelus(f, first, psum, dst, scale, done):
                act.wait_ge(psum, f * HT + first + 2)
                for j in (first, first + 1):
                    nc.scalar.activation(dst[:, j, :], f_bank[j % 2][:], ACT.Gelu,
                                         scale=scales_sb[:, scale, j:j + 1]).then_inc(done, 1)

            def feed_step(f, k):
                if k == 30:
                    act.wait_ge(ynT_psum, f + 1)
                    nc.scalar.copy(ynT[:], f_bank[0][:]).then_inc(ynT_done, 1)
                for pair in range(2):
                    if k == 32 + 5 * pair:
                        act.wait_ge(w1_psum, 2 * f + pair + 1)
                        for j in (0, 1):
                            last = nc.scalar.activation(hid_a[:, 2 * pair + j, :], f_bank[j][:], ACT.Silu,
                                                        scale=scales_sb[:, 0, 2 * pair + j:2 * pair + j + 1])
                        last.then_inc(gate_done, 1)
                if k in (49, 60):
                    gelus(f, 0 if k == 49 else 2, h1_psum, hid_b, 2, h1_done)

            def finish_step(g, k):
                if k in (8, 19):
                    gelus(g, 0 if k == 8 else 2, h2_psum, hid_a, 3, h2_done)

            def iteration(i, project, attend, feed, finish):
                for k in range(TILES):
                    if k % ST == (MAX_LAG + 1) % ST:
                        if k > MAX_LAG and attend:
                            copy_maxima(i, (k - MAX_LAG - 1) // ST)
                        if k < MAX_LAG and feed:
                            copy_maxima(i - 1, H - 1)
                    if k % 2 == EXP_LAG % 2:
                        if k >= EXP_LAG and attend:
                            exponential(i, k - EXP_LAG)
                        if k < EXP_LAG and feed:
                            exponential(i - 1, k - EXP_LAG + TILES)
                    if k % QT == 10:
                        if k >= QT and attend:
                            copy_output(i, k // QT - 1)
                        if k < QT and feed:
                            copy_output(i - 1, QUADS - 1)
                    if k == 13 and attend:
                        act.wait_ge(v_next_done, i + 1)
                        if begun(i):
                            act.wait_ge(pv_psum, i * QUADS)
                        act.wait_ge(stacks_clear, 4)
                        nc.scalar.copy(v_pad[:, :, :, 0:DH], v_next[:]).then_inc(v_pad_done, 1)
                    if project:
                        project_step(i + 1, k)
                    if finish:
                        finish_step(i - 2, k)
                    if feed:
                        feed_step(i - 1, k)

            stages(act, iteration)


def kernel(L0_attn_x, L0_attn_Wq, L0_attn_bq, L0_attn_Wv, L0_attn_bv, L0_attn_hyperplanes, L0_ffn_w1_w, L0_ffn_w1_s,
           L0_ffn_w2_w, L0_ffn_w2_s, L0_ffn_h1_w, L0_ffn_h1_s, L0_ffn_h2_w, L0_ffn_h2_s, L0_ffn_w3_w, L0_ffn_w3_s):
    import numpy as np
    from concourse import bacc
    from concourse.bass_utils import run_bass_kernel_spmd

    flat = np.ascontiguousarray
    wq = flat(np.asarray(L0_attn_Wq).reshape(H, DH, E).transpose(1, 0, 2).reshape(E, E).T)
    bq = flat(np.asarray(L0_attn_bq).reshape(H, DH).T.reshape(E))
    planes = np.asarray(L0_attn_hyperplanes)
    blocks = np.zeros((DH, H, NH, H), planes.dtype)
    bias = np.zeros((NH, H), planes.dtype)
    for h in range(H):
        blocks[:, h, :, h] = planes[:DH]
        bias[:, h] = planes[DH]
    scales = np.stack([np.asarray(s).reshape(HT, P) for s in (L0_ffn_w1_s, L0_ffn_w2_s, L0_ffn_h1_s, L0_ffn_h2_s)])
    scales = scales.transpose(2, 0, 1)
    arrays = {
        "x": flat(L0_attn_x), "wqT": wq, "bq": bq, "wvT": flat(np.asarray(L0_attn_Wv).T), "bv": flat(L0_attn_bv),
        "hyper_blocks": blocks.reshape(E, NH * H), "hyper_bias": bias.reshape(NH * H),
        "w1T": flat(np.asarray(L0_ffn_w1_w).T), "w2T": flat(np.asarray(L0_ffn_w2_w).T),
        "h1T": flat(np.asarray(L0_ffn_h1_w).T), "h2T": flat(np.asarray(L0_ffn_h2_w).T), "scales": flat(scales),
        "w3T": flat(np.asarray(L0_ffn_w3_w).T), "w3_s": flat(L0_ffn_w3_s),
    }
    nc = bacc.Bacc("TRN2", target_bir_lowering=False, num_devices=1)
    args = {n: nc.dram_tensor(f"in_{n}", a.shape, mybir.dt.from_np(a.dtype), kind="ExternalInput").ap()
            for n, a in arrays.items()}
    out = nc.dram_tensor("out", (BATCH, SEQ, E), FP32, kind="ExternalOutput").ap()
    sandwich_kernel(nc, **args, out=out)
    result = run_bass_kernel_spmd(nc, [{f"in_{n}": a for n, a in arrays.items()}], core_ids=[0])
    return result.results[0]["out"]
```

```python
from contextlib import ExitStack

import concourse.bass as bass
from concourse import mybir

FP32 = mybir.dt.float32
BF16 = mybir.dt.bfloat16
ALU = mybir.AluOpType
ACT = mybir.ActivationFunctionType
AXIS_X = mybir.AxisListType.X

P = 128
E = 128
H = 16
DH = E // H
NH = 6
BUCKETS = 2 ** NH
SEQ = 512
BATCH = 16
HID = 512
ST = SEQ // P
HT = HID // P
QUADS = H // 4
TILES = H * ST
QT = 4 * ST
PARTS = 3
KROWS = PARTS * PARTS * DH
VW = 32
EPS = 1e-5
GATE_SLOTS = (39, 41, 46, 48)
UP_SLOTS = (43, 45, 49, 54)
FIRST_HIDDEN_SLOTS = (57, 57, 57, 60, 60, 61, 63, 64, 65, 66, 67, 67, 69, 70, 70, 72)
SECOND_HIDDEN_SLOTS = (78, 80, 80, 81, 82, 82, 84, 85, 86, 87, 87, 88, 88, 94, 95, 95)
MULTIPLY_SLOTS = (42, 46, 52, 54)
OUTPUT_SLOTS = (98, 98, 99, 99)
FIRST_GELU_SLOTS = (65, 73)
SECOND_GELU_SLOTS = (85, 95)
F_BANKS = 3
GATE_BANKS = (1, 2, 2, 0)
UP_BANKS = (0, 1, 1, 2)
FIRST_HIDDEN_BANKS = (0, 1, 2, 0)
SECOND_HIDDEN_BANKS = (1, 2, 0, 1)
OUTPUT_BANK = 2
MAX_LAG = 6
PV_LAGS = (26, 27, 28, 28)
COPY_LAG = 29
TRANSPOSE_LAG = 32
DIVIDE_LAGS = (31, 32)
SHARED_LAG = 4
SUB_LAG = 8
EXP_LAG = 11
S_BANKS = 4
SHARED_HEADS = (0, 1, 6, 8, 12, 15)
RING = 16


def sandwich_kernel(nc, x, wqT, bq, wvT, bv, hyper_blocks, hyper_bias, w1T, w2T, h1T, h2T, scales, w3T, w3_s, out):
    ctx = ExitStack()
    with ctx:
        def sb(name, shape, dt=FP32):
            return ctx.enter_context(nc.sbuf_tensor(name, shape, dt))

        def bank(name):
            return ctx.enter_context(nc.psum_tensor(name, [P, SEQ], FP32))

        def sem(name):
            return ctx.enter_context(nc.semaphore(name))

        q_scratch = nc.dram_tensor("q_scratch", [BATCH, PARTS * DH, H * SEQ], BF16, kind="Internal").ap()
        bucket_scratch = nc.dram_tensor("bucket_scratch", [BATCH, H * SEQ], BF16, kind="Internal").ap()

        wq_sb = sb("wq_sb", [P, E])
        wv_sb = sb("wv_sb", [P, E])
        bq_sb = sb("bq_sb", [P, 1])
        bv_sb = sb("bv_sb", [P, E])
        hyper_sb = sb("hyper_sb", [P, NH * H])
        hbias_sb = sb("hbias_sb", [P, NH, H])
        pow2_sb = sb("pow2_sb", [P, NH, H])
        w1_sb = sb("w1_sb", [P, HID])
        w2_sb = sb("w2_sb", [P, HID])
        h1_sb = sb("h1_sb", [P, HT, HID])
        h2_sb = sb("h2_sb", [P, HT, HID])
        w3_sb = sb("w3_sb", [P, HT, E])
        scales_sb = sb("scales_sb", [P, 4, HT])
        w3s_sb = sb("w3s_sb", [P, E])
        ident = sb("ident", [P, P])
        ident16 = sb("ident16", [P, P], BF16)
        minus_half = sb("minus_half", [P, ST])

        x_in = sb("x_in", [P, ST, E])
        x_stats = sb("x_stats", [P, ST, 6])
        x_mv = sb("x_mv", [P, ST, 2])
        x_var = sb("x_var", [P, ST])
        x_rstd = sb("x_rstd", [P, ST])
        xnT = sb("xnT", [P, SEQ])
        qT = sb("qT", [P, SEQ])
        q_rest = xnT
        q_parts = sb("q_parts", [P, PARTS, SEQ], BF16)
        v_next = sb("v_next", [P, ST, H, DH])
        proj = sb("proj", [P, ST, NH, H])
        bcol_next = sb("bcol_next", [P, ST, H])
        bcol16 = sb("bcol16", [P, ST, H], BF16)
        brow16 = sb("brow16", [H, SEQ], BF16)

        stat_stack = sb("stat_stack", [P, 2, 4, SEQ], BF16)
        mov_stack = sb("mov_stack", [P, 2, 4, SEQ], BF16)
        brow = sb("brow", [P, 2, 4, SEQ], BF16)
        bcol = sb("bcol", [P, ST, H])
        coeff = sb("coeff", [P, 3, SEQ], BF16)
        logits = sb("logits", [P, RING, SEQ])
        rowmax = sb("rowmax", [P, TILES])
        max_row = sb("max_row", [P, 2, SEQ])
        probs = sb("probs", [P, 2, 4, ST, SEQ])
        v_pad = sb("v_pad", [P, ST, H, VW])
        oT = sb("oT", [P, SEQ])
        rden = sb("rden", [P, ST, 4])
        spare = sb("spare", [P, 1])
        table_warm = sb("table_warm", [P, 1])
        att = sb("att", [P, ST, E])

        x_res = sb("x_res", [P, ST, E])
        att_stats = sb("att_stats", [P, ST, 6])
        att_mv = sb("att_mv", [P, ST, 2])
        att_var = sb("att_var", [P, ST])
        att_rstd = sb("att_rstd", [P, ST])
        y1 = sb("y1", [P, ST, E])
        y1_kept = sb("y1_kept", [P, ST, E])
        end_stats = sb("end_stats", [P, ST, 6])
        end_mv = sb("end_mv", [P, ST, 2])
        end_var = sb("end_var", [P, ST])
        end_rstd = sb("end_rstd", [P, ST])
        ynT = sb("ynT", [P, SEQ])
        hid_a = sb("hid_a", [P, HT, SEQ])
        hid_b = sb("hid_b", [P, HT, SEQ])
        ffn = sb("ffn", [P, ST, E])

        s_bank = [bank(f"s_bank{n}") for n in range(S_BANKS)]
        f_bank = [bank(f"f_bank{n}") for n in range(F_BANKS)]
        aux_bank = bank("aux_bank")

        projection_in = sem("projection_in")
        ffn_in = sem("ffn_in")
        stacks_clear = sem("stacks_clear")
        v_pad_clear = sem("v_pad_clear")
        consts_made = sem("consts_made")
        x_loaded = sem("x_loaded")
        x_stats_done = sem("x_stats_done")
        x_mv_done = sem("x_mv_done")
        x_var_done = sem("x_var_done")
        x_rstd_done = sem("x_rstd_done")
        xn_done = sem("xn_done")
        xnT_psum = sem("xnT_psum")
        xnT_done = sem("xnT_done")
        q_psum = sem("q_psum")
        q_done = sem("q_done")
        v_psum = sem("v_psum")
        v_next_done = sem("v_next_done")
        proj_psum = sem("proj_psum")
        proj_done = sem("proj_done")
        bits_done = sem("bits_done")
        bcol_next_done = sem("bcol_next_done")
        bcol16_done = sem("bcol16_done")
        brow_psum = sem("brow_psum")
        brow_done = sem("brow_done")
        q_part_steps = sem("q_part_steps")
        scratch_written = sem("scratch_written")
        stack_loaded = [sem(f"stack_loaded{n}") for n in range(2)]
        bcol_done = sem("bcol_done")
        v_pad_done = sem("v_pad_done")
        scores_psum = sem("scores_psum")
        coeff_done = sem("coeff_done")
        logits_done = sem("logits_done")
        max_psum = sem("max_psum")
        max_row_done = sem("max_row_done")
        below_max_done = sem("below_max_done")
        shared_below_max_done = sem("shared_below_max_done")
        probs_done = sem("probs_done")
        pv_psum = sem("pv_psum")
        oT_done = sem("oT_done")
        o_psum = sem("o_psum")
        rden_done = sem("rden_done")
        att_done = sem("att_done")
        x_res_loaded = sem("x_res_loaded")
        att_stats_done = sem("att_stats_done")
        att_mv_done = sem("att_mv_done")
        att_var_done = sem("att_var_done")
        att_rstd_done = sem("att_rstd_done")
        normed_done = sem("normed_done")
        y1_done = sem("y1_done")
        y1_kept_done = sem("y1_kept_done")
        end_stats_done = sem("end_stats_done")
        end_mv_done = sem("end_mv_done")
        end_var_done = sem("end_var_done")
        end_rstd_done = sem("end_rstd_done")
        end_normed_done = sem("end_normed_done")
        yn_done = sem("yn_done")
        ynT_psum = sem("ynT_psum")
        ynT_done = sem("ynT_done")
        w1_psum = sem("w1_psum")
        gate_done = sem("gate_done")
        w2_psum = sem("w2_psum")
        h0_done = sem("h0_done")
        h1_psum = sem("h1_psum")
        h1_done = sem("h1_done")
        h2_psum = sem("h2_psum")
        h2_done = sem("h2_done")
        w3_psum = sem("w3_psum")
        ffn_done = sem("ffn_done")
        y2_done = sem("y2_done")
        out_stored = sem("out_stored")
        waited = sem("waited")

        PROJECTION_DMAS = 6
        FFN_DMAS = 7
        STACK_DMAS = 1 + PARTS + 1
        x_view = x.rearrange("b (s p) e -> b p s e", p=P)
        out_view = out.rearrange("b (s p) e -> b p s e", p=P)

        def apart(eng):
            eng.sem_inc(waited, 1)

        def by_vector(k):
            return k % ST == ST - 1 and k // ST in SHARED_HEADS

        def tile_bank(k):
            return s_bank[(k + (k + 1) // ST) % S_BANKS]

        def maxima_bank(h):
            k = (h * ST + MAX_LAG + 1) % TILES
            return s_bank[(k + (k + 1) // ST - 1) % S_BANKS]

        POOL_TILES = TILES - len(SHARED_HEADS)

        def pool_tiles(k):
            return sum(not by_vector(n) for n in range(k + 1))

        def quads_at(i, k, lag, attend, feed):
            quad, slot = divmod(k - lag, QT)
            if slot == 0 and quad >= 0 and attend:
                return [(i, quad)]
            if slot == 0 and quad < 0 and feed:
                return [(i - 1, quad + QUADS)]
            return []

        def begun(b):
            return not isinstance(b, int) or b > 0

        def stages(eng, iteration):
            iteration(-2, query=True, project=False, attend=False, feed=False, finish=False)
            iteration(-1, query=True, project=True, attend=False, feed=False, finish=False)
            iteration(0, query=True, project=True, attend=True, feed=False, finish=False)
            iteration(1, query=True, project=True, attend=True, feed=True, finish=False)
            with eng.Fori(2, BATCH - 2) as i:
                iteration(i, query=True, project=True, attend=True, feed=True, finish=True)
            iteration(BATCH - 2, query=False, project=True, attend=True, feed=True, finish=True)
            iteration(BATCH - 1, query=False, project=False, attend=True, feed=True, finish=True)
            iteration(BATCH, query=False, project=False, attend=False, feed=True, finish=True)
            iteration(BATCH + 1, query=False, project=False, attend=False, feed=False, finish=True)

        block = ctx.enter_context(nc.Block())

        @block.sync
        def _(sp):
            sp.dma_start(x_in[:], x_view[0]).then_inc(x_loaded, 16)
            for dst, src in (
                (wq_sb[:], wqT), (bq_sb[:], bq.rearrange("(p a) -> p a", a=1)),
                (wv_sb[:], wvT), (bv_sb[:], bv.rearrange("(a e) -> a e", a=1).broadcast_to([P, E])),
                (hyper_sb[:], hyper_blocks),
                (hbias_sb[:].rearrange("p n h -> p (n h)"),
                 hyper_bias.rearrange("(a e) -> a e", a=1).broadcast_to([P, NH * H])),
            ):
                sp.dma_start(dst, src).then_inc(projection_in, 16)
            def load_ffn_weights():
                for dst, src in (
                    (w1_sb[:], w1T), (w2_sb[:], w2T),
                    (h1_sb[:], h1T.rearrange("(k p) n -> p k n", p=P)),
                    (h2_sb[:], h2T.rearrange("(k p) n -> p k n", p=P)),
                    (scales_sb[:], scales),
                    (w3_sb[:], w3T.rearrange("(k p) n -> p k n", p=P)),
                    (w3s_sb[:], w3_s.rearrange("(a e) -> a e", a=1).broadcast_to([P, E])),
                ):
                    sp.dma_start(dst, src).then_inc(ffn_in, 16)

            def load_stacks(b, quad):
                slot = quad % 2
                cols = slice(quad * 4 * SEQ, (quad + 1) * 4 * SEQ)
                sp.dma_start(mov_stack[0:KROWS, slot].rearrange("p h n -> p (h n)"),
                             q_scratch[b][:, cols].unsqueeze(0).broadcast_to([PARTS, PARTS * DH, 4 * SEQ])
                             ).then_inc(stack_loaded[slot], 16)
                for i in range(PARTS):
                    rows = slice(i * PARTS * DH, (i + 1) * PARTS * DH)
                    sp.dma_start(stat_stack[rows, slot].rearrange("p h n -> p (h n)"),
                                 q_scratch[b][i * DH:(i + 1) * DH, cols].unsqueeze(0).broadcast_to(
                                     [PARTS, DH, 4 * SEQ])).then_inc(stack_loaded[slot], 16)
                sp.dma_start(brow[:, slot].rearrange("p h n -> p (h n)"),
                             bucket_scratch[b:b + 1, cols].broadcast_to([P, 4 * SEQ])
                             if isinstance(b, int) else
                             bucket_scratch[bass.ds(b, 1), cols].broadcast_to([P, 4 * SEQ])
                             ).then_inc(stack_loaded[slot], 16)

            def store_output(g):
                sp.wait_ge(y2_done, g + 1)
                apart(sp)
                sp.dma_start(out_view[g], ffn[:]).then_inc(out_stored, 16)

            def iteration(i, query, project, attend, feed, finish):
                p, b, f, g = i + 1, i, i - 1, i - 2
                if query and project:
                    sp.wait_ge(xnT_psum, p + 1)
                    apart(sp)
                    sp.dma_start(x_in[:], x_view[p + 1]).then_inc(x_loaded, 16)
                if attend:
                    if begun(b):
                        sp.wait_ge(logits_done, b * TILES)
                        apart(sp)
                    load_stacks(b, 1)
                    if not feed:
                        load_ffn_weights()
                    sp.wait_ge(logits_done, b * TILES + QT)
                    apart(sp)
                    load_stacks(b, 2)
                    if feed:
                        sp.wait_ge(ynT_psum, f + 1)
                        apart(sp)
                    sp.dma_start(x_res[:], x_view[b]).then_inc(x_res_loaded, 16)
                    sp.wait_ge(logits_done, b * TILES + 2 * QT)
                    apart(sp)
                    load_stacks(b, 3)
                if project:
                    for c in range(PARTS):
                        sp.wait_ge(q_part_steps, 4 * p + (1, 3, 4)[c])
                        apart(sp)
                        sp.dma_start(q_scratch[p][c * DH:(c + 1) * DH, :].rearrange("d (h n) -> (d h) n", h=H),
                                     q_parts[:, c, :]).then_inc(scratch_written, 16)
                    sp.wait_ge(brow_done, p + 1)
                    apart(sp)
                    sp.dma_start(bucket_scratch[p].rearrange("(h n) -> h n", h=H), brow16[:]).then_inc(scratch_written, 16)
                    sp.wait_ge(scratch_written, 4 * 16 * (p + 1))
                    apart(sp)
                    if not attend:
                        sp.wait_ge(stacks_clear, 2)
                if project:
                    if attend:
                        sp.wait_ge(logits_done, b * TILES + 3 * QT)
                        apart(sp)
                    load_stacks(p, 0)
                if finish:
                    store_output(g)
                if finish and query:
                    sp.wait_ge(out_stored, 16 * (g + 1))
                    apart(sp)

            stages(sp, iteration)
            sp.wait_ge(out_stored, 16 * BATCH)

        @block.tensor
        def _(pe):
            pe.wait_ge(projection_in, 16 * PROJECTION_DMAS)
            pe.wait_ge(consts_made, 4)

            def scores(b, k):
                h, t = divmod(k, ST)
                quad, hh = divmod(h, 4)
                if k % QT == 0:
                    pe.wait_ge(stack_loaded[quad % 2], 16 * STACK_DMAS * (2 * b + quad // 2 + 1))
                if k % ST == ST - 1:
                    if begun(b) or k >= 3:
                        pe.wait_ge(logits_done, b * TILES + k - 2)
                elif k % ST == 2 or begun(b) or k >= ST:
                    if k % ST == 2:
                        if begun(b) or k >= MAX_LAG:
                            pe.wait_ge(max_row_done, b * H + (k - MAX_LAG) // ST)
                    else:
                        pe.wait_ge(logits_done, b * TILES + k - 2)
                nc.tensor.matmul(tile_bank(k)[:], stat_stack[:, quad % 2, hh, t * P:(t + 1) * P],
                                 mov_stack[:, quad % 2, hh, :], start=True, stop=True).then_inc(scores_psum, 1)

            def spread_maxima(b, h):
                pe.wait_ge(logits_done, b * TILES + (h + 1) * ST)
                for t in range(ST):
                    last = nc.tensor.transpose(maxima_bank(h)[:, t * P:(t + 1) * P],
                                               rowmax[:, h * ST + t:h * ST + t + 1].broadcast_to([P, P]), ident[:])
                last.then_inc(max_psum, 1)

            def weigh_values(b, quad, j, query, project):
                if j == 0:
                    if quad == 0:
                        pe.wait_ge(v_pad_done, b + 1)
                    if quad == 0 and project:
                        pe.wait_ge(proj_done, b + 2)
                    elif quad == 1 and project:
                        pe.wait_ge(brow_done, b + 2)
                    elif quad == 2 and query:
                        pe.wait_ge(q_done, b + 3)
                    elif begun(b) or quad:
                        pe.wait_ge(att_done, b * QUADS + quad)
                    pe.wait_ge(probs_done, b * (TILES // 2) + (quad + 1) * QT // 2)
                for hh in range(4):
                    last = nc.tensor.matmul(aux_bank[hh * VW:(hh + 1) * VW, :], v_pad[:, j, quad * 4 + hh, :],
                                            probs[:, quad % 2, hh, j, :], start=(j == 0), stop=(j == ST - 1))
                if j == ST - 1:
                    last.then_inc(pv_psum, 1)

            def transpose_output(b, quad):
                pe.wait_ge(oT_done, b * QUADS + quad + 1)
                for t in range(ST):
                    last = nc.tensor.transpose(aux_bank[:, t * P:(t + 1) * P], oT[:, t * P:(t + 1) * P], ident[:])
                last.then_inc(o_psum, 1)

            def query_step(p, k, attend):
                if k == 51:
                    pe.wait_ge(xn_done, p + 1)
                    if attend:
                        pe.wait_ge(att_done, (p - 2) * QUADS + 2)
                    elif begun(p):
                        pe.wait_ge(brow_done, p)
                    for t in range(ST):
                        last = nc.tensor.transpose(aux_bank[:, t * P:(t + 1) * P], x_in[:, t, :], ident[:])
                    last.then_inc(xnT_psum, 1)
                if k == 54:
                    pe.wait_ge(xnT_done, p + 1)
                    nc.tensor.matmul(aux_bank[:], wq_sb[:], xnT[:], start=True, stop=True).then_inc(q_psum, 1)

            def project_step(p, k, attend):
                if k == 19:
                    pe.wait_ge(q_done, p + 1)
                    if begun(p - 1):
                        pe.wait_ge(att_done, (p - 1) * QUADS)
                    for t in range(ST):
                        last = nc.tensor.matmul(aux_bank[:, t * P:(t + 1) * P], xnT[:, t * P:(t + 1) * P], wv_sb[:],
                                                start=True, stop=True)
                    last.then_inc(v_psum, 1)
                if k == 23:
                    pe.wait_ge(v_next_done, p + 1)
                    for t in range(ST):
                        last = nc.tensor.matmul(aux_bank[:, t * NH * H:(t + 1) * NH * H], qT[:, t * P:(t + 1) * P],
                                                hyper_sb[:], start=True, stop=True)
                    last.then_inc(proj_psum, 1)
                if k == 36:
                    pe.wait_ge(consts_made, 5)
                    pe.wait_ge(bcol16_done, p + 1)
                    if attend:
                        pe.wait_ge(att_done, (p - 1) * QUADS + 1)
                    for t in range(ST):
                        last = nc.tensor.matmul(aux_bank[0:H, t * P:(t + 1) * P], bcol16[:, t, :], ident16[:],
                                                start=True, stop=True)
                    last.then_inc(brow_psum, 1)

            def ffn_step(f, slot, finish):
                if slot == 36:
                    pe.wait_ge(yn_done, f + 1)
                    for t in range(ST):
                        last = nc.tensor.transpose(f_bank[0][:, t * P:(t + 1) * P], x_res[:, t, :], ident[:])
                    last.then_inc(ynT_psum, 1)
                for j in range(HT):
                    col = slice(j * P, (j + 1) * P)
                    if slot == GATE_SLOTS[j]:
                        if j == 0:
                            pe.wait_ge(ynT_done, f + 1)
                        if j == 1 and finish:
                            pe.wait_ge(ffn_done, f)
                        if j == 2:
                            pe.wait_ge(gate_done, f * HT + 2)
                        if j == 3:
                            pe.wait_ge(h0_done, f * HT + 1)
                        nc.tensor.matmul(f_bank[GATE_BANKS[j]][:], w1_sb[:, col], ynT[:],
                                         start=True, stop=True).then_inc(w1_psum, 1)
                    if slot == UP_SLOTS[j]:
                        if j == 0:
                            pe.wait_ge(ynT_done, f + 1)
                        if j == 1:
                            pe.wait_ge(gate_done, f * HT + 1)
                        if j == 2:
                            pe.wait_ge(h0_done, f * HT + 2)
                        if j == 3:
                            pe.wait_ge(gate_done, f * HT + 3)
                        nc.tensor.matmul(f_bank[UP_BANKS[j]][:], w2_sb[:, col], ynT[:],
                                         start=True, stop=True).then_inc(w2_psum, 1)
                for n in range(HT * HT):
                    j, k = divmod(n, HT)
                    col = slice(j * P, (j + 1) * P)
                    if slot == FIRST_HIDDEN_SLOTS[n]:
                        if n == 0:
                            pe.wait_ge(h0_done, f * HT + HT)
                        if n == 3 * HT:
                            pe.wait_ge(h1_done, f * HT + 1)
                        last = nc.tensor.matmul(f_bank[FIRST_HIDDEN_BANKS[j]][:], h1_sb[:, k, col], hid_a[:, k, :],
                                                start=(k == 0), stop=(k == HT - 1))
                        if k == HT - 1:
                            last.then_inc(h1_psum, 1)
                    if slot == SECOND_HIDDEN_SLOTS[n]:
                        if n == 0:
                            pe.wait_ge(h1_done, f * HT + HT)
                        if n == 3 * HT:
                            pe.wait_ge(h2_done, f * HT + 1)
                        last = nc.tensor.matmul(f_bank[SECOND_HIDDEN_BANKS[j]][:], h2_sb[:, k, col], hid_b[:, k, :],
                                                start=(k == 0), stop=(k == HT - 1))
                        if k == HT - 1:
                            last.then_inc(h2_psum, 1)
                for t in range(ST):
                    if slot == OUTPUT_SLOTS[t]:
                        if t == 0:
                            pe.wait_ge(h2_done, f * HT + HT)
                        for j in range(HT):
                            last = nc.tensor.matmul(f_bank[OUTPUT_BANK][:, t * P:(t + 1) * P],
                                                    hid_a[:, j, t * P:(t + 1) * P], w3_sb[:, j, :],
                                                    start=(j == 0), stop=(j == HT - 1))
                        if t == ST - 1:
                            last.then_inc(w3_psum, 1)

            def iteration(i, query, project, attend, feed, finish):
                if feed and not finish:
                    pe.wait_ge(ffn_in, 16 * FFN_DMAS)
                for k in range(TILES):
                    if attend:
                        scores(i, k)
                    if k % ST == MAX_LAG % ST:
                        if k >= MAX_LAG and attend:
                            spread_maxima(i, (k - MAX_LAG) // ST)
                        if k < MAX_LAG and feed:
                            spread_maxima(i - 1, H - 1)
                    for j in range(ST):
                        for b, quad in quads_at(i, k, PV_LAGS[j], attend, feed):
                            weigh_values(b, quad, j, query, project)
                    for b, quad in quads_at(i, k, TRANSPOSE_LAG, attend, feed):
                        transpose_output(b, quad)
                    if query:
                        query_step(i + 2, k, attend)
                    if project:
                        project_step(i + 1, k, attend)
                    if finish:
                        ffn_step(i - 2, k + TILES, finish)
                    if feed:
                        ffn_step(i - 1, k, finish)

            stages(pe, iteration)

        @block.vector
        def _(dve):
            for n in range(NH):
                last = nc.vector.memset(pow2_sb[:, n, :], float(2 ** n))
            last.then_inc(consts_made, 1)
            nc.vector.memset(stat_stack[:], 0.0).then_inc(stacks_clear, 1)
            nc.vector.memset(mov_stack[:], 0.0).then_inc(stacks_clear, 1)

            def coefficients(b, k):
                h, t = divmod(k, ST)
                nc.vector.tensor_scalar(coeff[:, k % 3, :], brow[:, h // 4 % 2, h % 4, :], bcol[:, t, h:h + 1],
                                        float(BUCKETS - 2), ALU.is_equal, ALU.add).then_inc(coeff_done, 1)

            def attend_tile(b, k):
                dve.wait_ge(scores_psum, b * TILES + k + 1)
                dve.wait_ge(coeff_done, b * TILES + k + 1)
                if k % 2 == 0 and (begun(b) or k >= RING):
                    dve.wait_ge(probs_done, b * (TILES // 2) + (k - RING) // 2 + 1)
                if k + 1 < TILES:
                    if (k + 1) % QT == 0:
                        quad = (k + 1) // QT
                        dve.wait_ge(stack_loaded[quad % 2], 16 * STACK_DMAS * (2 * b + quad // 2 + 1))
                    coefficients(b, k + 1)
                else:
                    nc.vector.memset(spare[:], 1.0)
                nc.vector.tensor_tensor_reduce(
                    out=logits[:, k % RING, :], in0=tile_bank(k)[:], in1=coeff[:, k % 3, :], scale=float(E) ** -0.5,
                    scalar=-3.0e38, op0=ALU.mult, op1=ALU.max, accum_out=rowmax[:, k:k + 1]).then_inc(logits_done, 1)

            def moments(src, stats, mv, stats_done, mv_done, step, n):
                if step == 0:
                    for t in range(ST):
                        last = nc.vector.bn_stats(stats[:, t, :], src[:, t, :])
                    last.then_inc(stats_done, 1)
                else:
                    dve.wait_ge(stats_done, n)
                    apart(dve)
                    for t in range(ST):
                        last = nc.vector.bn_aggr(mv[:, t, :], stats[:, t, :])
                    last.then_inc(mv_done, 1)

            def normalise(dst, src, mv, rstd, done):
                for t in range(ST):
                    last = nc.vector.tensor_scalar(dst[:, t, :], src[:, t, :], mv[:, t, 0:1], rstd[:, t:t + 1],
                                                   ALU.subtract, ALU.mult)
                last.then_inc(done, 1)

            def output_step(b, quad, step):
                o4 = aux_bank[:].rearrange("p (t h w) -> p t h w", t=ST, w=VW)
                if step == 0:
                    dve.wait_ge(o_psum, b * QUADS + quad + 1)
                    nc.vector.reciprocal(rden[:].unsqueeze(3), o4[:, :, :, DH:DH + 1]).then_inc(rden_done, 1)
                else:
                    dve.wait_ge(rden_done, b * QUADS + quad + 1)
                    nc.vector.tensor_tensor(
                        att[:, :, quad * 4 * DH:(quad + 1) * 4 * DH].rearrange("p t (h d) -> p t h d", d=DH),
                        o4[:, :, :, 0:DH], rden[:].unsqueeze(3).broadcast_to([P, ST, 4, DH]),
                        ALU.mult).then_inc(att_done, 1)

            def query_step(p, k):
                if k == 29:
                    dve.wait_ge(x_loaded, 16 * (p + 1))
                    moments(x_in, x_stats, x_mv, x_stats_done, x_mv_done, 0, p + 1)
                if k == 30:
                    moments(x_in, x_stats, x_mv, x_stats_done, x_mv_done, 1, p + 1)
                if k == 42:
                    dve.wait_ge(x_rstd_done, p + 1)
                    normalise(x_in, x_in, x_mv, x_rstd, xn_done)

            def project_step(p, k):
                if k == 19:
                    dve.wait_ge(v_psum, p + 1)
                    if begun(p):
                        dve.wait_ge(v_pad_done, p)
                    if isinstance(p, int) and p == 0:
                        dve.wait_ge(projection_in, 16 * PROJECTION_DMAS)
                    nc.vector.tensor_tensor(v_next[:].rearrange("p t h d -> p t (h d)"),
                                            aux_bank[:].rearrange("p (t e) -> p t e", t=ST),
                                            bv_sb[:].unsqueeze(1).broadcast_to([P, ST, E]), ALU.add).then_inc(v_next_done, 1)
                if k == 23:
                    dve.wait_ge(proj_psum, p + 1)
                    nc.vector.tensor_tensor(proj[:].rearrange("p t n h -> p t (n h)"),
                                            aux_bank[:, 0:ST * NH * H].rearrange("p (t e) -> p t e", t=ST),
                                            hbias_sb[:].rearrange("p n h -> p (n h)").unsqueeze(1).broadcast_to([P, ST, NH * H]),
                                            ALU.add).then_inc(proj_done, 1)
                if k == 24:
                    dve.wait_ge(proj_done, p + 1)
                    nc.vector.scalar_tensor_tensor(out=proj[:].rearrange("p t n h -> p t (n h)"),
                                                   in0=proj[:].rearrange("p t n h -> p t (n h)"), scalar=0.0,
                                                   in1=pow2_sb[:].rearrange("p n h -> p (n h)").unsqueeze(1).broadcast_to([P, ST, NH * H]),
                                                   op0=ALU.is_ge, op1=ALU.mult).then_inc(bits_done, 1)
                if k == 26:
                    dve.wait_ge(bits_done, p + 1)
                    nc.vector.reduce_sum(bcol_next[:], proj[:].rearrange("p t n h -> p t h n"), AXIS_X).then_inc(bcol_next_done, 1)
                if k == 19:
                    dve.wait_ge(q_part_steps, 4 * p + 1)
                    nc.vector.tensor_tensor(q_rest[:], qT[:], q_parts[:, 0, :], ALU.subtract).then_inc(q_part_steps, 1)
                if k == 30:
                    dve.wait_ge(q_part_steps, 4 * p + 3)
                    nc.vector.tensor_tensor(q_parts[:, 2, :], q_rest[:], q_parts[:, 1, :],
                                            ALU.subtract).then_inc(q_part_steps, 1)

            def feed_step(f, k):
                if k == 17:
                    dve.wait_ge(att_done, QUADS * (f + 1))
                    moments(att, att_stats, att_mv, att_stats_done, att_mv_done, 0, 2 * f + 1)
                if k == 18:
                    moments(att, att_stats, att_mv, att_stats_done, att_mv_done, 1, 2 * f + 1)
                if k == 23:
                    dve.wait_ge(att_rstd_done, 2 * f + 1)
                    if begun(f):
                        dve.wait_ge(y1_kept_done, f)
                    normalise(y1, att, att_mv, att_rstd, normed_done)
                if k == 23:
                    dve.wait_ge(normed_done, f + 1)
                    dve.wait_ge(x_res_loaded, 16 * (f + 1))
                    nc.vector.tensor_tensor(y1[:], y1[:], x_res[:], ALU.add).then_inc(y1_done, 1)
                if k == 24:
                    dve.wait_ge(y1_done, f + 1)
                    moments(y1, att_stats, att_mv, att_stats_done, att_mv_done, 0, 2 * f + 2)
                if k == 26:
                    moments(y1, att_stats, att_mv, att_stats_done, att_mv_done, 1, 2 * f + 2)
                if k == 33:
                    dve.wait_ge(att_rstd_done, 2 * f + 2)
                    normalise(x_res, y1, att_mv, att_rstd, yn_done)
                for j, slot in enumerate(MULTIPLY_SLOTS):
                    if k == slot:
                        dve.wait_ge(w2_psum, f * HT + j + 1)
                        dve.wait_ge(gate_done, f * HT + j + 1)
                        nc.vector.scalar_tensor_tensor(
                            out=hid_a[:, j, :], in0=f_bank[UP_BANKS[j]][:], scalar=scales_sb[:, 1, j:j + 1],
                            in1=hid_a[:, j, :], op0=ALU.mult, op1=ALU.mult).then_inc(h0_done, 1)

            def finish_step(g, k):
                if k == 37:
                    dve.wait_ge(w3_psum, g + 1)
                    if isinstance(g, int) and g:
                        dve.wait_ge(out_stored, 16 * g)
                    nc.vector.tensor_tensor(ffn[:], f_bank[OUTPUT_BANK][:].rearrange("p (t e) -> p t e", t=ST),
                                            w3s_sb[:].unsqueeze(1).broadcast_to([P, ST, E]), ALU.mult).then_inc(ffn_done, 1)
                if k == 56:
                    dve.wait_ge(ffn_done, g + 1)
                    moments(ffn, end_stats, end_mv, end_stats_done, end_mv_done, 0, g + 1)
                if k == 56:
                    moments(ffn, end_stats, end_mv, end_stats_done, end_mv_done, 1, g + 1)
                if k == 59:
                    dve.wait_ge(end_rstd_done, g + 1)
                    normalise(ffn, ffn, end_mv, end_rstd, end_normed_done)
                if k == 60:
                    dve.wait_ge(end_normed_done, g + 1)
                    dve.wait_ge(y1_kept_done, g + 1)
                    nc.vector.tensor_tensor(ffn[:], ffn[:], y1_kept[:], ALU.add).then_inc(y2_done, 1)

            def subtract(b, k):
                h = k // ST
                dve.wait_ge(max_row_done, b * H + h + 1)
                nc.vector.tensor_tensor(logits[:, k % RING, :], max_row[:, h % 2, :], logits[:, k % RING, :],
                                        ALU.subtract).then_inc(shared_below_max_done, 1)

            def iteration(i, query, project, attend, feed, finish):
                if query and not project:
                    dve.wait_ge(consts_made, 4)
                    nc.vector.tensor_copy(ident16[:], ident[:]).then_inc(consts_made, 1)
                if feed and not finish:
                    dve.wait_ge(ffn_in, 16 * FFN_DMAS)
                if attend:
                    dve.wait_ge(bcol_next_done, i + 1)
                    nc.vector.tensor_copy(bcol[:], bcol_next[:]).then_inc(bcol_done, 1)
                    dve.wait_ge(stack_loaded[0], 16 * STACK_DMAS * (2 * i + 1))
                    dve.wait_ge(bcol_done, i + 1)
                    coefficients(i, 0)
                for k in range(TILES):
                    if attend:
                        attend_tile(i, k)
                    if k >= SHARED_LAG and attend and by_vector(k - SHARED_LAG):
                        subtract(i, k - SHARED_LAG)
                    if k < SHARED_LAG and feed and by_vector(k - SHARED_LAG + TILES):
                        subtract(i - 1, k - SHARED_LAG + TILES)
                    for step in (0, 1):
                        for b, quad in quads_at(i, k, DIVIDE_LAGS[step], attend, feed):
                            output_step(b, quad, step)
                    if project:
                        project_step(i + 1, k)
                    if query:
                        query_step(i + 2, k)
                    if finish:
                        finish_step(i - 2, k)
                    if feed:
                        feed_step(i - 1, k)

            stages(dve, iteration)

        @block.gpsimd
        def _(pool):
            nc.gpsimd.memset(ident[:], 0.0).then_inc(consts_made, 1)
            nc.gpsimd.memset(minus_half[:], -0.5).then_inc(consts_made, 1)
            nc.gpsimd.memset(v_pad[:], 0.0).then_inc(v_pad_clear, 1)
            pool.wait_ge(v_pad_clear, 1)
            nc.gpsimd.memset(v_pad[:, :, :, DH:DH + 1], 1.0).then_inc(v_pad_clear, 1)
            pool.wait_ge(consts_made, 1)
            nc.gpsimd.affine_select(out=ident[:], in_=ident[:], compare_op=ALU.not_equal, fill=1.0, base=0,
                                    pattern=[[-1, P]], channel_multiplier=1).then_inc(consts_made, 1)
            pool.wait_ge(consts_made, 4)

            def rstd(mv, var, out_, ready, var_done, done, n):
                pool.wait_ge(ready, n)
                apart(pool)
                nc.gpsimd.tensor_scalar(var[:], mv[:, :, 1], EPS, 1.0, ALU.add, ALU.mult).then_inc(var_done, 1)
                pool.wait_ge(var_done, n)
                apart(pool)
                nc.gpsimd.tensor_tensor(out_[:], var[:], minus_half[:], ALU.pow).then_inc(done, 1)

            def subtract(b, k):
                h, t = divmod(k, ST)
                if t == 0:
                    pool.wait_ge(max_row_done, b * H + h + 1)
                pool.wait_ge(logits_done, b * TILES + k + 1)
                nc.gpsimd.tensor_tensor(logits[:, k % RING, :], max_row[:, h % 2, :], logits[:, k % RING, :],
                                        ALU.subtract).then_inc(below_max_done, 1)

            def iteration(i, query, project, attend, feed, finish):
                p, b, f, g = i + 1, i, i - 1, i - 2
                for k in range(TILES):
                    if k >= SUB_LAG and attend and not by_vector(k - SUB_LAG):
                        subtract(b, k - SUB_LAG)
                    if k < SUB_LAG and feed and not by_vector(k - SUB_LAG + TILES):
                        subtract(f, k - SUB_LAG + TILES)
                    if query and k == 37:
                        rstd(x_mv, x_var, x_rstd, x_mv_done, x_var_done, x_rstd_done, p + 2)
                    if finish and k == 57:
                        rstd(end_mv, end_var, end_rstd, end_mv_done, end_var_done, end_rstd_done, g + 1)
                    if feed and k == 20:
                        rstd(att_mv, att_var, att_rstd, att_mv_done, att_var_done, att_rstd_done, 2 * f + 1)
                    if feed and k == 29:
                        rstd(att_mv, att_var, att_rstd, att_mv_done, att_var_done, att_rstd_done, 2 * f + 2)

            stages(pool, iteration)

        @block.scalar
        def _(act):
            act.wait_ge(consts_made, 4)
            nc.scalar.activation(table_warm[:], ident[:, 0:1], ACT.Exp)
            act.wait_ge(projection_in, 16 * PROJECTION_DMAS)

            def copy_maxima(b, h):
                act.wait_ge(max_psum, b * H + h + 1)
                nc.scalar.copy(max_row[:, h % 2, :], maxima_bank(h)[:]).then_inc(max_row_done, 1)

            def exponential(b, k):
                h, t = divmod(k, ST)
                act.wait_ge(below_max_done, b * POOL_TILES + pool_tiles(k + 1))
                if by_vector(k + 1):
                    act.wait_ge(shared_below_max_done, (b + 1) * len(SHARED_HEADS) if k + 2 == TILES else
                                b * len(SHARED_HEADS) + SHARED_HEADS.index(h) + 1)
                nc.scalar.activation(probs[:, h // 4 % 2, h % 4, t:t + 2, :], logits[:, k % RING:k % RING + 2, :],
                                     ACT.Exp, scale=-1.0).then_inc(probs_done, 1)

            def copy_output(b, quad):
                act.wait_ge(pv_psum, b * QUADS + quad + 1)
                if begun(b) or quad:
                    act.wait_ge(o_psum, b * QUADS + quad)
                nc.scalar.copy(oT[:], aux_bank[:]).then_inc(oT_done, 1)

            def query_step(p, k):
                if k == 50:
                    act.wait_ge(xnT_psum, p + 1)
                    if begun(p):
                        act.wait_ge(q_part_steps, 4 * p)
                    nc.scalar.copy(xnT[:], aux_bank[:]).then_inc(xnT_done, 1)
                if k == 52:
                    act.wait_ge(q_psum, p + 1)
                    nc.scalar.activation(qT[:], aux_bank[:], ACT.Identity, bias=bq_sb[:]).then_inc(q_done, 1)
                if k == 58:
                    act.wait_ge(q_done, p + 1)
                    if begun(p):
                        act.wait_ge(scratch_written, 4 * 16 * p)
                    nc.scalar.copy(q_parts[:, 0, :], qT[:]).then_inc(q_part_steps, 1)

            def project_step(p, k):
                if k == 24:
                    act.wait_ge(q_part_steps, 4 * p + 2)
                    nc.scalar.copy(q_parts[:, 1, :], q_rest[:]).then_inc(q_part_steps, 1)
                if k == 27:
                    act.wait_ge(bcol_next_done, p + 1)
                    nc.scalar.copy(bcol16[:], bcol_next[:]).then_inc(bcol16_done, 1)
                if k == 40:
                    act.wait_ge(brow_psum, p + 1)
                    nc.scalar.copy(brow16[:], aux_bank[0:H, :]).then_inc(brow_done, 1)

            def ffn_step(f, slot):
                if slot == 14 + TILES:
                    if isinstance(f, int) and f:
                        act.wait_ge(y2_done, f)
                    act.wait_ge(yn_done, f + 1)
                    nc.scalar.copy(y1_kept[:], y1[:]).then_inc(y1_kept_done, 1)
                if slot == 37:
                    act.wait_ge(ynT_psum, f + 1)
                    nc.scalar.copy(ynT[:], f_bank[0][:]).then_inc(ynT_done, 1)
                for pair in range(2):
                    if slot == GATE_SLOTS[2 * pair + 1] + 1:
                        act.wait_ge(w1_psum, f * HT + 2 * pair + 2)
                        for j in (2 * pair, 2 * pair + 1):
                            nc.scalar.activation(hid_a[:, j, :], f_bank[GATE_BANKS[j]][:], ACT.Silu,
                                                 scale=scales_sb[:, 0, j:j + 1]).then_inc(gate_done, 1)
                    if slot == FIRST_GELU_SLOTS[pair]:
                        act.wait_ge(h1_psum, f * HT + 2 * pair + 2)
                        for j in (2 * pair, 2 * pair + 1):
                            nc.scalar.activation(hid_b[:, j, :], f_bank[FIRST_HIDDEN_BANKS[j]][:], ACT.Gelu,
                                                 scale=scales_sb[:, 2, j:j + 1]).then_inc(h1_done, 1)
                    if slot == SECOND_GELU_SLOTS[pair]:
                        act.wait_ge(h2_psum, f * HT + 2 * pair + 2)
                        for j in (2 * pair, 2 * pair + 1):
                            nc.scalar.activation(hid_a[:, j, :], f_bank[SECOND_HIDDEN_BANKS[j]][:], ACT.Gelu,
                                                 scale=scales_sb[:, 3, j:j + 1]).then_inc(h2_done, 1)

            def iteration(i, query, project, attend, feed, finish):
                if feed and not finish:
                    act.wait_ge(ffn_in, 16 * FFN_DMAS)
                for k in range(TILES):
                    if k % ST == MAX_LAG % ST:
                        if k >= MAX_LAG and attend:
                            copy_maxima(i, (k - MAX_LAG) // ST)
                        if k < MAX_LAG and feed:
                            copy_maxima(i - 1, H - 1)
                    if k % 2 == EXP_LAG % 2:
                        if k >= EXP_LAG and attend:
                            exponential(i, k - EXP_LAG)
                        if k < EXP_LAG and feed:
                            exponential(i - 1, k - EXP_LAG + TILES)
                    for b, quad in quads_at(i, k, COPY_LAG, attend, feed):
                        copy_output(b, quad)
                    if k == 15 and attend:
                        act.wait_ge(v_next_done, i + 1)
                        if begun(i):
                            act.wait_ge(pv_psum, i * QUADS)
                        act.wait_ge(v_pad_clear, 2)
                        nc.scalar.copy(v_pad[:, :, :, 0:DH], v_next[:]).then_inc(v_pad_done, 1)
                    if project:
                        project_step(i + 1, k)
                    if query:
                        query_step(i + 2, k)
                    if finish:
                        ffn_step(i - 2, k + TILES)
                    if feed:
                        ffn_step(i - 1, k)

            stages(act, iteration)


def kernel(L0_attn_x, L0_attn_Wq, L0_attn_bq, L0_attn_Wv, L0_attn_bv, L0_attn_hyperplanes, L0_ffn_w1_w, L0_ffn_w1_s,
           L0_ffn_w2_w, L0_ffn_w2_s, L0_ffn_h1_w, L0_ffn_h1_s, L0_ffn_h2_w, L0_ffn_h2_s, L0_ffn_w3_w, L0_ffn_w3_s):
    import numpy as np
    from concourse import bacc
    from concourse.bass_utils import run_bass_kernel_spmd

    flat = np.ascontiguousarray
    wq = flat(np.asarray(L0_attn_Wq).reshape(H, DH, E).transpose(1, 0, 2).reshape(E, E).T)
    bq = flat(np.asarray(L0_attn_bq).reshape(H, DH).T.reshape(E))
    planes = np.asarray(L0_attn_hyperplanes)
    blocks = np.zeros((DH, H, NH, H), planes.dtype)
    bias = np.zeros((NH, H), planes.dtype)
    for h in range(H):
        blocks[:, h, :, h] = planes[:DH]
        bias[:, h] = planes[DH]
    scales = np.stack([np.asarray(s).reshape(HT, P) for s in (L0_ffn_w1_s, L0_ffn_w2_s, L0_ffn_h1_s, L0_ffn_h2_s)])
    scales = scales.transpose(2, 0, 1)
    arrays = {
        "x": flat(L0_attn_x), "wqT": wq, "bq": bq, "wvT": flat(np.asarray(L0_attn_Wv).T), "bv": flat(L0_attn_bv),
        "hyper_blocks": blocks.reshape(E, NH * H), "hyper_bias": bias.reshape(NH * H),
        "w1T": flat(np.asarray(L0_ffn_w1_w).T), "w2T": flat(np.asarray(L0_ffn_w2_w).T),
        "h1T": flat(np.asarray(L0_ffn_h1_w).T), "h2T": flat(np.asarray(L0_ffn_h2_w).T), "scales": flat(scales),
        "w3T": flat(np.asarray(L0_ffn_w3_w).T), "w3_s": flat(L0_ffn_w3_s),
    }
    nc = bacc.Bacc("TRN2", target_bir_lowering=False, num_devices=1)
    args = {n: nc.dram_tensor(f"in_{n}", a.shape, mybir.dt.from_np(a.dtype), kind="ExternalInput").ap()
            for n, a in arrays.items()}
    out = nc.dram_tensor("out", (BATCH, SEQ, E), FP32, kind="ExternalOutput").ap()
    sandwich_kernel(nc, **args, out=out)
    result = run_bass_kernel_spmd(nc, [{f"in_{n}": a for n, a in arrays.items()}], core_ids=[0])
    return result.results[0]["out"]
```
